# Optimizing a Trainium2 kernel written in Bass

```python
import numpy as np
import jax
import jax.numpy as jnp

def _softmax(x, axis=-1):
    return jax.nn.softmax(x, axis=axis)

def _gelu(x):
    return jax.nn.gelu(x, approximate=True)

def _silu(x):
    return jax.nn.silu(x)

def _sigmoid(x):
    return jax.nn.sigmoid(x)

def _layernorm(x, axis=-1, eps=1e-05):
    m = jnp.mean(x, axis=axis, keepdims=True)
    v = jnp.var(x, axis=axis, keepdims=True)
    return (x - m) / jnp.sqrt(v + eps)

def _scatter_add(tgt, idx, src, axis=0):
    return tgt.at[idx].add(src)

def _segment_sum(src, seg, n):
    return jax.ops.segment_sum(src, seg, n)
kernel_name = 'mk_seq_postln_d1_jaxref_r8_ca8631'

def setup_inputs(seed: int=0):
    np.random.seed(seed)
    _w = jnp.asarray

    def _L0_attn_setup():
        import jax, jax.numpy as jnp
        from jax import lax
        import numpy as np
        D = 128
        H = 16
        DK = D // 2 // H
        DV = D // H
        GATE_NORM = 16.0
        SCALE = DK ** (-0.5)
        EPS = 1e-05

        def _split_heads(x, dh):
            B, L, _ = x.shape
            return x.reshape(B, L, H, dh).transpose(0, 2, 1, 3)

        def _gla_scan(q, k, v, log_gate):
            B = q.shape[0]
            qt = jnp.moveaxis(q, 2, 0)
            kt = jnp.moveaxis(k, 2, 0)
            vt = jnp.moveaxis(v, 2, 0)
            gt = jnp.exp(jnp.moveaxis(log_gate, 2, 0))

            def step(state, inp):
                qq, kk, vv, gg = inp
                state = state * gg[..., None] + kk[..., :, None] * vv[..., None, :]
                out = jnp.einsum('bhd,bhde->bhe', qq, state)
                return (state, out)
            init = jnp.zeros((B, H, DK, DV), dtype=q.dtype)
            _, outs = lax.scan(step, init, (qt, kt, vt, gt))
            return jnp.moveaxis(outs, 0, 2)
        key = jax.random.key(seed)
        ks = jax.random.split(key, 10)
        s = 0.02
        return {'inputs': jax.random.normal(ks[0], (4, 512, D), dtype=jnp.float32), 'Wq': jax.random.normal(ks[1], (D, D // 2), dtype=jnp.float32) * s, 'Wk': jax.random.normal(ks[2], (D, D // 2), dtype=jnp.float32) * s, 'Wg1': jax.random.normal(ks[3], (D, 16), dtype=jnp.float32) * s, 'Wg2': jax.random.normal(ks[4], (16, D // 2), dtype=jnp.float32) * s, 'Wv': jax.random.normal(ks[5], (D, D), dtype=jnp.float32) * s, 'Wg': jax.random.normal(ks[6], (D, D), dtype=jnp.float32) * s, 'bg': jax.random.normal(ks[7], (D,), dtype=jnp.float32) * s, 'Wo': jax.random.normal(ks[8], (D, D), dtype=jnp.float32) * s}
    _L0_attn_in = _L0_attn_setup()

    def _L0_ffn_setup():
        import jax, jax.numpy as jnp
        import numpy as np
        K = 2
        key = jax.random.key(seed)
        k1, k2, k3, k4 = jax.random.split(key, 4)
        B, S, D, E, F = (2, 128, 128, 8, 512)
        x = jax.random.normal(k1, (B, S, D), dtype=jnp.float32)
        gate_w = jax.random.normal(k2, (E, D), dtype=jnp.float32) * (1.0 / np.sqrt(D))
        w1 = jax.random.normal(k3, (E, D, F), dtype=jnp.float32) * (1.0 / np.sqrt(D))
        w2 = jax.random.normal(k4, (E, F, D), dtype=jnp.float32) * (1.0 / np.sqrt(F))
        return {'x': x, 'gate_w': gate_w, 'w1': w1, 'w2': w2}
    _L0_ffn_in = _L0_ffn_setup()
    _d = {'L0_attn_inputs': _L0_attn_in['inputs'], 'L0_attn_Wq': _L0_attn_in['Wq'], 'L0_attn_Wk': _L0_attn_in['Wk'], 'L0_attn_Wg1': _L0_attn_in['Wg1'], 'L0_attn_Wg2': _L0_attn_in['Wg2'], 'L0_attn_Wv': _L0_attn_in['Wv'], 'L0_attn_Wg': _L0_attn_in['Wg'], 'L0_attn_bg': _L0_attn_in['bg'], 'L0_attn_Wo': _L0_attn_in['Wo'], 'L0_ffn_gate_w': _L0_ffn_in['gate_w'], 'L0_ffn_w1': _L0_ffn_in['w1'], 'L0_ffn_w2': _L0_ffn_in['w2']}
    _x0 = _d['L0_attn_inputs']
    _d['L0_attn_inputs'] = jax.random.normal(jax.random.fold_in(jax.random.key(seed), 1), (32, 256, 128), dtype=_x0.dtype)
    del _x0
    return _d

def reference(L0_attn_inputs, L0_attn_Wq, L0_attn_Wk, L0_attn_Wg1, L0_attn_Wg2, L0_attn_Wv, L0_attn_Wg, L0_attn_bg, L0_attn_Wo, L0_ffn_gate_w, L0_ffn_w1, L0_ffn_w2):

    def _L0_attn_ref(inputs, Wq, Wk, Wg1, Wg2, Wv, Wg, bg, Wo):
        import jax, jax.numpy as jnp
        from jax import lax
        import numpy as np
        D = 128
        H = 16
        DK = D // 2 // H
        DV = D // H
        GATE_NORM = 16.0
        SCALE = DK ** (-0.5)
        EPS = 1e-05

        def _split_heads(x, dh):
            B, L, _ = x.shape
            return x.reshape(B, L, H, dh).transpose(0, 2, 1, 3)

        def _gla_scan(q, k, v, log_gate):
            B = q.shape[0]
            qt = jnp.moveaxis(q, 2, 0)
            kt = jnp.moveaxis(k, 2, 0)
            vt = jnp.moveaxis(v, 2, 0)
            gt = jnp.exp(jnp.moveaxis(log_gate, 2, 0))

            def step(state, inp):
                qq, kk, vv, gg = inp
                state = state * gg[..., None] + kk[..., :, None] * vv[..., None, :]
                out = jnp.einsum('bhd,bhde->bhe', qq, state)
                return (state, out)
            init = jnp.zeros((B, H, DK, DV), dtype=q.dtype)
            _, outs = lax.scan(step, init, (qt, kt, vt, gt))
            return jnp.moveaxis(outs, 0, 2)
        B, L, _ = inputs.shape
        q = _split_heads(inputs @ Wq, DK)
        k = _split_heads(inputs @ Wk * SCALE, DK)
        kg = _split_heads(inputs @ Wg1 @ Wg2, DK)
        v = _split_heads(inputs @ Wv, DV)
        gate = jax.nn.silu(inputs @ Wg + bg)
        log_gate = jax.nn.log_sigmoid(kg) / GATE_NORM
        o = _gla_scan(q, k, v, log_gate)
        mu = jnp.mean(o, axis=-1, keepdims=True)
        var = jnp.var(o, axis=-1, keepdims=True)
        o = (o - mu) * lax.rsqrt(var + EPS)
        o = o.transpose(0, 2, 1, 3).reshape(B, L, D)
        return gate * o @ Wo

    def _L0_ffn_ref(x, gate_w, w1, w2):
        import jax, jax.numpy as jnp
        import numpy as np
        K = 2
        D = x.shape[-1]
        xt = x.reshape(-1, D)
        T = xt.shape[0]
        E = gate_w.shape[0]
        logits = jnp.einsum('td,ed->te', xt, gate_w)
        w_topk, sel = jax.lax.top_k(logits, K)
        w_topk = jax.nn.softmax(w_topk.astype(jnp.float32), axis=-1).astype(x.dtype)
        combine = jnp.zeros((T, E), dtype=x.dtype)
        combine = combine.at[jnp.arange(T)[:, None], sel].add(w_topk)
        h = jax.nn.silu(jnp.einsum('td,edf->tef', xt, w1))
        y = jnp.einsum('tef,efd->ted', h, w2)
        out = jnp.einsum('ted,te->td', y, combine)
        return out.reshape(x.shape)
    x = L0_attn_inputs
    x = _layernorm(x + _L0_attn_ref(x, L0_attn_Wq, L0_attn_Wk, L0_attn_Wg1, L0_attn_Wg2, L0_attn_Wv, L0_attn_Wg, L0_attn_bg, L0_attn_Wo), axis=-1)
    x = _layernorm(x + _L0_ffn_ref(x, L0_ffn_gate_w, L0_ffn_w1, L0_ffn_w2), axis=-1)
    return x

_drawn_inputs = setup_inputs


def setup_inputs(seed=0):
    import zlib

    import numpy as np

    out = dict(_drawn_inputs(seed))
    spreads = {}
    factors = {'L0_attn_Wg1': 34.134, 'L0_attn_Wg2': 31.43, 'L0_attn_bg': 4.259}
    for name, (base, spread) in spreads.items():
        noise = np.random.default_rng([zlib.crc32(name.encode()), seed]).standard_normal(out[name].shape)
        drawn = base * np.exp(spread * noise) if base else spread * noise
        out[name] = jnp.asarray(drawn.astype(out[name].dtype))
    for name, factor in factors.items():
        out[name] = (out[name] * factor).astype(out[name].dtype)
    return out
```

```python
from contextlib import ExitStack

import concourse.bass as bass
import numpy as np
from concourse import mybir

F32 = mybir.dt.float32
BF16 = mybir.dt.bfloat16
I32 = mybir.dt.int32
U32 = mybir.dt.uint32
ALU = mybir.AluOpType
ACT = mybir.ActivationFunctionType
AX = mybir.AxisListType

P = 128
D = 128
H, DK, DV = 16, 4, 8
HK = H * DK
NB, L = 32, 256
TOKENS = NB * L
E, F = 8, 512
FT = F // P
EPS = 1e-5
GATE_NORM = 16.0

UNIT = 512
TL = UNIT // P
UNITS = TOKENS // UNIT
BU = UNIT // L
G = 4

TS = 256
ST = TS // P
TILES = (2 * TOKENS - E) // TS + E
REGION = TOKENS + TS
DUMP = E * REGION
ROW = D + 4
F_DEST, F_EXPERT, F_DW, F_W1 = D, D + 1, D + 2, D + 3
NOWHERE = 1.0e6

CG = 8
TT = TOKENS // P
GROUPS = TT // CG


class Step:

    def __init__(self, i, c):
        self.i, self.c = i, c

    def __add__(self, k):
        return Step(self.i, self.c + k)

    def __sub__(self, k):
        return Step(self.i, self.c - k)

    @property
    def n(self):
        return self.i * 2 + self.c

    @property
    def par(self):
        return self.c % 2

    @property
    def half(self):
        return self.i + self.c // 2


def wait(eng, sem, value):
    if isinstance(value, int) and value <= 0:
        return
    eng.wait_ge(sem, value)


def steps(eng, first, loop_from, loop_to, last, body):
    for s in range(first, loop_from):
        body(Step(s // 2, s % 2), s)
    with eng.Fori(loop_from // 2, loop_to // 2) as i:
        body(Step(i, 0), None)
        body(Step(i, 1), None)
    for s in range(loop_to, last + 1):
        body(Step(s // 2, s % 2), s)


def has(s, k, count):
    return s is None or 0 <= s - k < count


def build(nc, x, Wk, Wq, Wg1, Wg2, WvG, Wg, bg, Wo, gate_wT, w1, w2, ident, center, tri, iota8, out):
    with ExitStack() as ctx:
        def sb(name, shape, dt=F32):
            return ctx.enter_context(nc.sbuf_tensor(name, shape, dt))

        def sem(name):
            return ctx.enter_context(nc.semaphore(name))

        rows = nc.dram_tensor("expert_rows", (DUMP + TS, ROW), F32).ap()
        ybuf = nc.dram_tensor("expert_out", (2 * TOKENS, D), F32).ap()

        ps = ctx.enter_context(nc.psum_tensor("ps", [P, 8, 512], F32))
        ring = [ps[:, b, :] for b in range(4)]
        tbank, obank, wbank = ps[:, 4, :], ps[:, 5, :], ps[:, 6, :]
        lbank = ps[:, 7, 0:TL * E]
        pbank = ps[:, 7, 64:64 + TL * E]

        idn = sb("idn", [P, P])
        cen = sb("cen", [P, G, P])
        tri_f = sb("tri_f", [P, 2, P])
        tri_b = sb("tri_b", [P, 2, P], BF16)
        iota_e = sb("iota_e", [P, 3, E])
        wk = sb("wk", [P, 2, HK])
        wq = sb("wq", [P, 2, HK])
        wg1 = sb("wg1", [P, 16])
        wg1t = sb("wg1t", [16, P])
        wg2 = sb("wg2", [16, HK])
        wdec = sb("wdec", [P, 2, HK])
        wv = sb("wv", [P, G, 2, H])
        wvr = sb("wvr", [P, G, 2, H, DK])
        wg = sb("wg", [P, D])
        bgc = sb("bgc", [P, 1])
        nbg = sb("nbg", [P, 1])
        eps = sb("eps", [P, 2])
        wo = sb("wo", [P, D])
        gw = sb("gw", [P, E])
        w1s = sb("w1s", [P, E, F])
        w2s = sb("w2s", [P, E, FT, D])

        xs = sb("xs", [P, 2, TL, D])
        xr = sb("xr", [P, 2, TL, D])
        xt = sb("xt", [P, 2, UNIT])
        ks = sb("ks", [P, 2, UNIT])
        qs = sb("qs", [P, 2, UNIT])
        dabs = sb("dabs", [P, UNIT])
        dexp = sb("dexp", [P, UNIT])
        dln = sb("dln", [P, UNIT])
        dls = sb("dls", [P, UNIT])
        dec = sb("dec", [P, 2, UNIT])
        kv = sb("kv", [P, G, UNIT])
        state = sb("state", [P, 2, G, UNIT])
        qst = sb("qst", [P, 2, G, UNIT])
        ge = sb("ge", [P, UNIT])
        ge1 = sb("ge1", [P, UNIT])
        gr = sb("gr", [P, UNIT])
        gate = sb("gate", [P, 2, UNIT])
        osq = sb("osq", [P, UNIT])
        hss = sb("hss", [P, TL * H])
        hln = sb("hln", [P, TL * H])
        hrs = sb("hrs", [P, TL * H])
        on = sb("on", [P, 2, UNIT])
        go = sb("go", [P, UNIT])
        rsum = sb("rsum", [P, TL, D])
        st6 = sb("st6", [P, TL, 6])
        mv = sb("mv", [P, TL, 2])
        lln = sb("lln", [P, TL])
        lrs = sb("lrs", [P, TL])
        ys = sb("ys", [P, 2, TL, ROW])
        yres = sb("yres", [P, TT, D])
        yt = sb("yt", [P, UNIT])
        m8 = sb("m8", [P, TL, 8])
        i8 = sb("i8", [P, TL, 8], U32)
        idf = sb("idf", [P, TL, 2])
        oneh = sb("oneh", [P, TL, 2, E])
        mask = sb("mask", [P, TL, E], BF16)
        msum = sb("msum", [P, E])
        carry = sb("carry", [P, E], BF16)
        wd = sb("wd", [P, TL])
        we = sb("we", [P, TL])
        we1 = sb("we1", [P, TL])
        w0 = sb("w0", [P, TL])
        w1f = sb("w1f", [P, TL])
        sbase = sb("sbase", [P, TL, E])
        sprod = sb("sprod", [P, TL, 2, E])
        slotf = sb("slotf", [P, TL * 2])
        slot = sb("slot", [P, 2, TL * 2], I32)
        dest_i = sb("dest_i", [P, TT], I32)
        dest = sb("dest", [P, TT])

        padrow = sb("padrow", [P, ROW])
        iop_i = sb("iop_i", [P, 1], I32)
        iop = sb("iop", [P, 1])
        iot_i = sb("iot_i", [P, TILES], I32)
        iot = sb("iot", [P, TILES])
        cnt = sb("cnt", [P, E])
        padf = sb("padf", [P, 2, E])
        padi = sb("padi", [P, 2, E], I32)
        cnti = sb("cnti", [P, E], I32)
        cnts = sb("cnts", [P, E], I32)
        ntf = sb("ntf", [P, E])
        tend = sb("tend", [P, E])
        tstart = sb("tstart", [P, E])
        tbase = sb("tbase", [P, E])
        flat_q = qst[:].rearrange("p u g t -> p (u g t)")
        tge, tgs, tin, tin2 = (
            flat_q[:, k * TILES * E:(k + 1) * TILES * E].rearrange("p (t e) -> p t e", e=E) for k in range(4))
        texp = sb("texp", [P, TILES])
        tvalid = sb("tvalid", [P, TILES])
        trow = sb("trow", [P, TILES])
        trow2 = sb("trow2", [P, TILES])
        row_i = sb("row_i", [P, TILES], I32)
        exp_i = sb("exp_i", [P, TILES], I32)

        xl = sb("xl", [P, 2, ST, ROW])
        xbt = sb("xbt", [P, 2, TS])
        wb1 = state[:, 0].rearrange("p (u a) (f m) -> p u (a f) m", u=2, f=4)[:, :, 0:FT, :]
        wb2 = state[:, 1].rearrange("p (u a) (f m) -> p u (a f) m", u=2, f=4)[:, :, 0:FT, :]
        hb = kv[:].rearrange("p (u a) (f t) -> p u (a f) t", u=2, f=2)
        ytb = sb("ytb", [P, 2, TS])
        yo = sb("yo", [P, 2, ST, D])
        fsel = sb("fsel", [P, ST])
        fwd = sb("fwd", [P, ST])
        fw = sb("fw", [P, 2, ST])
        fdst = sb("fdst", [P, 2, ST], I32)

        def reuse(buf, k):
            return buf[:, k].rearrange("p g (a t d) -> p (g a) t d", a=1, d=D).rearrange(
                "p (u g) t d -> p u (g t) d", u=2)

        y0, y1, ya, co = reuse(state, 0), reuse(state, 1), reuse(qst, 0), reuse(qst, 1)
        cs6 = sb("cs6", [P, CG, 6])
        cmv = sb("cmv", [P, 2, CG, 2])
        cln = sb("cln", [P, CG])
        crs = sb("crs", [P, CG])

        const_in = sem("const_in")
        expert_in = sem("expert_in")
        dump_in = sem("dump_in")
        x_in = [sem("x_in0"), sem("x_in1")]
        xr_in = [sem("xr_in0"), sem("xr_in1")]
        setup_pool = sem("setup_pool")
        setup_dve = sem("setup_dve")
        nbg_sb = sem("nbg_sb")
        pool_passed, dve_passed = sem("pool_passed"), sem("dve_passed")
        wg1t_ps = sem("wg1t_ps")
        wdec_ps = sem("wdec_ps")
        xt_ps, xt_sb = sem("xt_ps"), sem("xt_sb")
        k_ps, d_ps, q_ps, z_ps, v_ps = (sem(s) for s in ("k_ps", "d_ps", "q_ps", "z_ps", "v_ps"))
        k_sb, q_sb = sem("k_sb"), sem("q_sb")
        dchain, ls_sb, dec_sb = sem("dchain"), sem("ls_sb"), sem("dec_sb")
        kv_sb, scan_sb, qst_sb = sem("kv_sb"), sem("scan_sb"), sem("qst_sb")
        ge_sb, gchain, gate_sb = sem("ge_sb"), sem("gchain"), sem("gate_sb")
        o_ps, osq_sb, hss_sb, hln_sb, hrs_sb, on_sb = (
            sem(s) for s in ("o_ps", "osq_sb", "hss_sb", "hln_sb", "hrs_sb", "on_sb"))
        on_t, go_sb, wo_ps = sem("on_t"), sem("go_sb"), sem("wo_ps")
        r_sb, lchain, lln_sb, lrs_sb, y_sb = (sem(s) for s in ("r_sb", "lchain", "lln_sb", "lrs_sb", "y_sb"))
        y_t, yt_sb, lg_ps, yres_sb = sem("y_t"), sem("yt_sb"), sem("lg_ps"), sem("yres_sb")
        rchain, mask_sb, wd_sb, we_sb, wchain = (
            sem(s) for s in ("rchain", "mask_sb", "wd_sb", "we_sb", "wchain"))
        carry_sb, pos_ps, schain, slot_sb, field_sb, dest_sb = (
            sem(s) for s in ("carry_sb", "pos_ps", "schain", "slot_sb", "field_sb", "dest_sb"))
        scattered = [sem("scattered0"), sem("scattered1")]
        cnt_ps, tchain, pad_sb, table_sb, padded = (
            sem(s) for s in ("cnt_ps", "tchain", "pad_sb", "table_sb", "padded"))
        rows_in = [sem("rows_in0"), sem("rows_in1")]
        bx_ps, bx_sb, bw_sb = sem("bx_ps"), sem("bx_sb"), sem("bw_sb")
        h_ps, h_sb, by_ps, by_sb, yo_ps, yo_sb = (
            sem(s) for s in ("h_ps", "h_sb", "by_ps", "by_sb", "yo_ps", "yo_sb"))
        fchain, field_read = sem("fchain"), sem("field_read")
        returned = [sem("returned0"), sem("returned1")]
        y_in = [sem("y_in0"), sem("y_in1")]
        ya_sb, cchain, cln_sb, crs_sb, co_sb = (sem(s) for s in ("ya_sb", "cchain", "cln_sb", "crs_sb", "co_sb"))
        stored = [sem("stored0"), sem("stored1")]

        CONSTS = [(idn[:], ident), (cen[:], center), (tri_f[:], tri), (iota_e[:], iota8),
                  (wk[:, 0, :], Wk), (wk[:, 1, :], Wk), (wq[:, 0, :], Wq), (wq[:, 1, :], Wq),
                  (wg1[:], Wg1), (wg2[:], Wg2), (wv[:], WvG), (wg[:], Wg), (bgc[:], bg),
                  (wo[:], Wo), (gw[:], gate_wT)]
        SA = (0, 4, UNITS - 2, UNITS + 1)
        SB = (0, 4, TILES - 1 - (TILES - 1) % 2, TILES + 1)
        SC = (0, 4, GROUPS, GROUPS)

        block = ctx.enter_context(nc.Block())

        def settle(eng):
            eng.sem_inc(pool_passed if eng is nc.gpsimd else dve_passed, 1)

        @block.sync
        def _(sp):
            def load_x(s, k):
                if not has(k, 0, UNITS):
                    return
                wait(sp, xt_ps, s.n - 1)
                sp.dma_start(xs[:, s.par], x[bass.ds(s.n, 1)].rearrange("u p t d -> (u p) t d")
                             ).then_inc(x_in[s.par], 16)

            def load_xr(s, k):
                if not has(k, 0, UNITS):
                    return
                wait(sp, r_sb, s.n - 1)
                sp.dma_start(xr[:, s.par], x[bass.ds(s.n, 1)].rearrange("u p t d -> (u p) t d")
                             ).then_inc(xr_in[s.par], 16)

            load_x(Step(0, 0), 0)
            for dst, src in CONSTS:
                sp.dma_start(dst, src).then_inc(const_in, 16)
            load_x(Step(0, 1), 1)
            load_xr(Step(0, 0), 0)
            load_xr(Step(0, 1), 1)
            sp.dma_start(w1s[:], w1.rearrange("e d f -> d e f")).then_inc(expert_in, 16)
            for e in range(E):
                sp.dma_start(w2s[:, e], w2[e].rearrange("(t p) d -> p t d", p=P)).then_inc(expert_in, 16)
            sp.wait_ge(setup_pool, 4)
            for k in range(ST):
                sp.dma_start(rows[DUMP + k * P:DUMP + (k + 1) * P, :], padrow[:]).then_inc(dump_in, 16)

            def body(s, k):
                load_x(s, k)
                load_xr(s, k)
            steps(sp, 2, 2, UNITS, UNITS - 1, body)

            for q in scattered:
                sp.wait_ge(q, UNITS // 2 * TL * 2 * 16)
            sp.wait_ge(padded, 16 * ST * E)
            sp.wait_ge(dump_in, 16 * ST)
            sp.wait_ge(table_sb, 2)

            def load_rows(s, k):
                if not has(k, 0, TILES):
                    return
                wait(sp, bx_ps, s.n - 1)
                wait(sp, field_read, s.n - 1)
                at = sp.value_load(row_i[0:1, bass.ds(s.n, 1)], min_val=0, max_val=DUMP)
                sp.dma_start(xl[:, s.par], rows[bass.ds(at, TS), :].rearrange("(t p) d -> p t d", p=P)
                             ).then_inc(rows_in[s.par], 16)
            steps(sp, 0, 2, TILES - 1, TILES - 1, load_rows)

            sp.wait_ge(returned[0], (TILES + 1) // 2 * ST * 16)
            sp.wait_ge(returned[1], TILES // 2 * ST * 16)
            yv = ybuf.rearrange("(c p t) d -> c p (t d)", c=2, p=P)
            ov = out.rearrange("(t p) d -> p t d", p=P)

            def load_y(s, k):
                if has(k, 0, GROUPS):
                    wait(sp, ya_sb, s.n - 1)
                    for c, buf in enumerate((y0, y1)):
                        sp.dma_start(buf[:, s.par].rearrange("p t d -> p (t d)"),
                                     yv[c, :, bass.ds(s.n * (CG * D), CG * D)]).then_inc(y_in[s.par], 16)

            steps(sp, 0, 2, GROUPS, GROUPS - 1, load_y)

        @block.gpsimd
        def _(pool):
            nc.gpsimd.memset(padrow[:, 0:D], 0.0).then_inc(setup_pool, 1)
            nc.gpsimd.memset(padrow[:, D:ROW], 0.0).then_inc(setup_pool, 1)
            pool.wait_ge(setup_pool, 2)
            nc.gpsimd.memset(padrow[:, F_DEST:F_DEST + 1], NOWHERE).then_inc(setup_pool, 1)
            nc.gpsimd.memset(padrow[:, F_EXPERT:F_EXPERT + 1], -1.0).then_inc(setup_pool, 1)
            nc.gpsimd.iota(iop_i[:], [[0, 1]], base=0, channel_multiplier=1).then_inc(setup_pool, 1)
            nc.gpsimd.iota(iot_i[:], [[1, TILES]], base=0, channel_multiplier=0).then_inc(setup_pool, 1)
            nc.gpsimd.iota(dest_i[:], [[1, TT]], base=TOKENS, channel_multiplier=TT).then_inc(setup_pool, 1)

            def products(s, k):
                if not has(k, 0, UNITS):
                    return
                pool.wait_ge(q_sb, s.n + 1)
                for g in range(G):
                    pool.wait_ge(scan_sb, s.n * (G * BU) + (g + 1) * BU)
                    if g == 0:
                        wait(pool, o_ps, s.n - 1)
                    nc.gpsimd.tensor_tensor(qst[:, s.par, g], qs[:, s.par], state[:, s.par, g],
                                            ALU.mult).then_inc(qst_sb, 1)

            def scatter(s, k):
                if not has(k, 0, UNITS):
                    return
                pool.wait_ge(y_sb, (s.n + 1) * TL)
                pool.wait_ge(field_sb, (s.n + 1) * 3)
                pool.wait_ge(dest_sb, s.n + 1)
                pool.wait_ge(slot_sb, s.n + 1)
                settle(pool)
                for t in range(TL):
                    for c in range(2):
                        m = 2 * t + c
                        pool.indirect_dma_start(
                            out=rows, out_offset=bass.IndirectOffsetOnAxis(ap=slot[:, s.par, m:m + 1], axis=0),
                            in_=ys[:, s.par, t, :], in_offset=None).then_inc(scattered[s.par], 16)

            def body(s, k):
                products(s, k)
                scatter(s - 2, None if k is None else k - 2)
            steps(pool, *SA, body)

            pool.wait_ge(pad_sb, 1)
            for c in range(ST):
                for e in range(E):
                    pool.indirect_dma_start(
                        out=rows, out_offset=bass.IndirectOffsetOnAxis(ap=padi[:, c, e:e + 1], axis=0),
                        in_=padrow[:], in_offset=None).then_inc(padded, 16)

            def give_back(s, k):
                if not has(k, 2, TILES):
                    return
                s = s - 2
                pool.wait_ge(yo_sb, (s.n + 1) * ST)
                settle(pool)
                for t in range(ST):
                    pool.indirect_dma_start(
                        out=ybuf, out_offset=bass.IndirectOffsetOnAxis(ap=fdst[:, s.par, t:t + 1], axis=0),
                        in_=yo[:, s.par, t, :], in_offset=None, bounds_check=2 * TOKENS - 1,
                        oob_is_err=False).then_inc(returned[s.par], 16)
            steps(pool, *SB, give_back)

            def add_up(s, k):
                if not has(k, 0, GROUPS):
                    return
                pool.wait_ge(y_in[s.par], (s.half + 1) * 32)
                wait(pool, co_sb, (s.n - 1) * CG)
                nc.gpsimd.tensor_tensor(ya[:, s.par], y0[:, s.par], y1[:, s.par], ALU.add).then_inc(ya_sb, 1)
            steps(pool, *SC, add_up)

        @block.scalar
        def _(act):
            act.wait_ge(const_in, 16 * len(CONSTS))
            nc.scalar.activation(nbg[:], bgc[:], ACT.Copy, scale=-1.0).then_inc(nbg_sb, 1)
            act.wait_ge(nbg_sb, 1)
            act.wait_ge(setup_dve, 9 + G)

            def copy_xt(s, k):
                if has(k, 0, UNITS):
                    act.wait_ge(xt_ps, s.n + 1)
                    wait(act, v_ps, (s.n - 1) * G)
                    nc.scalar.activation(xt[:, s.par], tbank, ACT.Copy).then_inc(xt_sb, 1)

            def decay_a(s, k):
                if not has(k, 0, UNITS):
                    return
                act.wait_ge(d_ps, s.n + 1)
                nc.scalar.activation(dabs[:], ring[1], ACT.Abs).then_inc(dchain, 1)
                act.wait_ge(dchain, s.n * 3 + 1)
                nc.scalar.activation(dexp[:], dabs[:], ACT.Exp, scale=-1.0).then_inc(dchain, 1)
                act.wait_ge(dchain, s.n * 3 + 2)
                wait(act, ls_sb, s.n)
                nc.scalar.activation(dln[:], dexp[:], ACT.Ln, bias=1.0).then_inc(dchain, 1)

            def copy_k(s, k):
                if has(k, 0, UNITS):
                    act.wait_ge(k_ps, s.n + 1)
                    wait(act, kv_sb, (s.n - 1) * G)
                    nc.scalar.activation(ks[:, s.par], ring[0], ACT.Copy, scale=DK ** -0.5).then_inc(k_sb, 1)

            def decay_b(s, k):
                if has(k, 0, UNITS):
                    act.wait_ge(ls_sb, s.n + 1)
                    wait(act, scan_sb, (s.n - 1) * (G * BU))
                    nc.scalar.activation(dec[:, s.par], dls[:], ACT.Exp, scale=1.0 / GATE_NORM).then_inc(dec_sb, 1)

            def copy_q(s, k):
                if has(k, 0, UNITS):
                    act.wait_ge(q_ps, s.n + 1)
                    wait(act, qst_sb, (s.n - 1) * G)
                    nc.scalar.activation(qs[:, s.par], ring[2], ACT.Copy).then_inc(q_sb, 1)

            def gate_exp(s, k):
                if has(k, 0, UNITS):
                    act.wait_ge(z_ps, s.n + 1)
                    wait(act, gate_sb, s.n)
                    nc.scalar.activation(ge[:], ring[3], ACT.Exp, bias=nbg[:], scale=-1.0).then_inc(ge_sb, 1)

            def square(s, k):
                if has(k, 0, UNITS):
                    act.wait_ge(o_ps, s.n + 1)
                    wait(act, on_sb, s.n)
                    nc.scalar.activation(osq[:], obank, ACT.Square).then_inc(osq_sb, 1)

            def root(src, tmp, dst, bias, tmp_sb, dst_sb, n):
                nc.scalar.activation(tmp, src, ACT.Ln, bias=bias).then_inc(tmp_sb, 1)
                act.wait_ge(tmp_sb, n + 1)
                nc.scalar.activation(dst, tmp, ACT.Exp, scale=-0.5).then_inc(dst_sb, 1)

            def head_root(s, k):
                if has(k, 0, UNITS):
                    act.wait_ge(hss_sb, s.n + 1)
                    wait(act, on_sb, s.n)
                    root(hss[:], hln[:], hrs[:], eps[:, 1:2], hln_sb, hrs_sb, s.n)

            def layer_root(s, k):
                if has(k, 0, UNITS):
                    act.wait_ge(lchain, (s.n + 1) * 8)
                    wait(act, y_sb, s.n * TL)
                    root(mv[:, :, 1], lln[:], lrs[:], eps[:, 0:1], lln_sb, lrs_sb, s.n)

            def copy_yt(s, k):
                if has(k, 0, UNITS):
                    act.wait_ge(y_t, s.n + 1)
                    wait(act, lg_ps, s.n)
                    nc.scalar.activation(yt[:], tbank, ACT.Copy).then_inc(yt_sb, 1)

            def keep_y(s, k):
                if has(k, 0, UNITS):
                    act.wait_ge(y_sb, (s.n + 1) * TL)
                    nc.scalar.activation(yres[:, bass.ds(s.n * TL, TL), :], ys[:, s.par, :, 0:D],
                                         ACT.Copy).then_inc(yres_sb, 1)

            def weight_exp(s, k):
                if has(k, 0, UNITS):
                    act.wait_ge(wd_sb, s.n + 1)
                    wait(act, field_sb, s.n * 3)
                    nc.scalar.activation(we[:], wd[:], ACT.Exp).then_inc(we_sb, 1)

            copy_xt(Step(0, 0), 0)

            def body(s, k):
                k1, k2, kn = (None,) * 3 if k is None else (k - 1, k - 2, k + 1)
                decay_a(s, k)
                copy_k(s, k)
                copy_yt(s - 2, k2)
                square(s - 1, k1)
                decay_b(s, k)
                copy_q(s, k)
                head_root(s - 1, k1)
                gate_exp(s, k)
                keep_y(s - 2, k2)
                weight_exp(s - 2, k2)
                copy_xt(s + 1, kn)
                layer_root(s - 1, k1)
            steps(act, *SA, body)

            def silu(s, k):
                if not has(k, 0, TILES):
                    return
                for b in range(2):
                    act.wait_ge(h_ps, s.n * 2 + b + 1)
                    if b == 0:
                        wait(act, by_ps, s.n - 1)
                    nc.scalar.activation(hb[:, s.par, 2 * b:2 * b + 2, :].rearrange("p f t -> p (f t)"),
                                         ps[:, 2 * s.par + b, :], ACT.Silu).then_inc(h_sb, 1)

            def weigh(s, k):
                if not has(k, 0, TILES):
                    return
                act.wait_ge(yo_ps, s.n + 1)
                act.wait_ge(fchain, (s.n + 1) * 3)
                act.wait_ge(field_read, s.n + 1)
                wait(act, returned[s.par], s.half * (ST * 16))
                for t in range(ST):
                    nc.scalar.activation(yo[:, s.par, t, :], ps[:, 6, t * D:(t + 1) * D], ACT.Copy,
                                         scale=fw[:, s.par, t:t + 1]).then_inc(yo_sb, 1)

            def bodyb(s, k):
                silu(s, k)
                weigh(s - 2, None if k is None else k - 2)
            steps(act, *SB, bodyb)

            ov = out.rearrange("(t p) d -> p t d", p=P)

            def final_root(s, k):
                if has(k, 0, GROUPS):
                    act.wait_ge(cchain, (s.n + 1) * (2 * CG + 1))
                    wait(act, co_sb, s.n * CG)
                    root(cmv[:, s.par, :, 1], cln[:], crs[:], eps[:, 0:1], cln_sb, crs_sb, s.n)

            def store(s, k):
                if has(k, 0, GROUPS):
                    act.wait_ge(co_sb, (s.n + 1) * CG)
                    act.dma_start(ov[:, bass.ds(s.n * CG, CG), :], co[:, s.par]).then_inc(stored[s.par], 16)

            def bodyc(s, k):
                final_root(s, k)
                store(s - 1, None if k is None else k - 1)
            steps(act, *SC, bodyc)
            for q in stored:
                act.wait_ge(q, GROUPS // 2 * 16)

        @block.tensor
        def _(pe):
            pe.wait_ge(const_in, 16 * len(CONSTS))

            def turn(bank, src, tiles, done):
                for t in range(tiles):
                    mm = nc.tensor.transpose(bank[:, t * P:(t + 1) * P], src(t), idn[:])
                mm.then_inc(done, 1)

            def turn_x(s, k):
                if has(k, 0, UNITS):
                    pe.wait_ge(x_in[s.par], (s.half + 1) * 16)
                    wait(pe, go_sb, s.n - 1)
                    turn(tbank, lambda t: xs[:, s.par, t, :], TL, xt_ps)

            def project(s, bank, w, done):
                nc.tensor.matmul(ring[bank], w, xt[:, s.par], start=True, stop=True).then_inc(done, 1)

            def flat(w):
                return w.rearrange("p a b -> p (a b)")

            def keys(s, k):
                if has(k, 0, UNITS):
                    pe.wait_ge(xt_sb, s.n + 1)
                    wait(pe, kv_sb, (s.n - 1) * G + 2)
                    project(s, 1, flat(wdec[:]), d_ps)
                    project(s, 0, flat(wk[:]), k_ps)

            def queries(s, k):
                if has(k, 0, UNITS):
                    wait(pe, kv_sb, s.n * G)
                    project(s, 2, flat(wq[:]), q_ps)
                    project(s, 3, wg[:], z_ps)

            def values(s, k, g):
                if has(k, 0, UNITS):
                    pe.wait_ge((k_sb, ls_sb, q_sb, gate_sb)[g], s.n + 1)
                    project(s, g, wvr[:, g].rearrange("p j h k -> p (j h k)"), v_ps)

            def heads(s, k):
                if not has(k, 0, UNITS):
                    return
                pe.wait_ge(qst_sb, (s.n + 1) * G)
                wait(pe, on_sb, s.n)
                for t in range(TL):
                    for g in range(G):
                        mm = nc.tensor.matmul(obank[:, t * P:(t + 1) * P], qst[:, s.par, g, t * P:(t + 1) * P],
                                              cen[:, g, :], start=(g == 0), stop=(g == G - 1))
                mm.then_inc(o_ps, 1)

            def turn_o(s, k):
                if has(k, 0, UNITS):
                    pe.wait_ge(on_sb, s.n + 1)
                    wait(pe, yt_sb, s.n)
                    turn(tbank, lambda t: on[:, s.par, t * P:(t + 1) * P], TL, on_t)

            def project_o(s, k):
                if not has(k, 0, UNITS):
                    return
                pe.wait_ge(go_sb, s.n + 1)
                wait(pe, r_sb, s.n)
                for t in range(TL):
                    mm = nc.tensor.matmul(wbank[:, t * P:(t + 1) * P], go[:, t * P:(t + 1) * P], wo[:],
                                          start=True, stop=True)
                mm.then_inc(wo_ps, 1)

            def turn_y(s, k):
                if has(k, 0, UNITS):
                    pe.wait_ge(y_sb, (s.n + 1) * TL)
                    turn(tbank, lambda t: ys[:, s.par, t, 0:D], TL, y_t)

            def logits(s, k):
                if not has(k, 0, UNITS):
                    return
                pe.wait_ge(yt_sb, s.n + 1)
                wait(pe, schain, s.n * 3)
                for t in range(TL):
                    mm = nc.tensor.matmul(lbank[:, t * E:(t + 1) * E], yt[:, t * P:(t + 1) * P], gw[:],
                                          start=True, stop=True)
                mm.then_inc(lg_ps, 1)

            def positions(s, k):
                if not has(k, 0, UNITS):
                    return
                pe.wait_ge(mask_sb, s.n + 1)
                wait(pe, carry_sb, s.n + 1)
                m = mask[:].rearrange("p t e -> p (t e)")
                nc.tensor.matmul(pbank, tri_b[:, 0, :], m, start=True, stop=False)
                for t in range(1, TL):
                    nc.tensor.matmul(pbank[:, t * E:], tri_b[:, 1, :], m[:, 0:(TL - t) * E],
                                     start=False, stop=False)
                for t in range(TL):
                    mm = nc.tensor.matmul(pbank[:, t * E:(t + 1) * E], tri_b[:, 1, :], carry[:],
                                          start=False, stop=(t == TL - 1))
                mm.then_inc(pos_ps, 1)

            nc.tensor.transpose(tbank[0:16, 0:P], wg1[:], idn[:]).then_inc(wg1t_ps, 1)
            pe.wait_ge(setup_dve, 1)
            nc.tensor.matmul(obank[:, 0:HK], wg1t[:], wg2[:], start=True, stop=True).then_inc(wdec_ps, 1)
            turn_x(Step(0, 0), 0)
            pe.wait_ge(setup_dve, 9 + G)

            def body(s, k):
                k1, k2, kn = (None,) * 3 if k is None else (k - 1, k - 2, k + 1)
                keys(s, k)
                turn_y(s - 2, k2)
                heads(s - 1, k1)
                queries(s, k)
                logits(s - 2, k2)
                values(s, k, 0)
                values(s, k, 1)
                turn_o(s - 1, k1)
                values(s, k, 2)
                values(s, k, 3)
                positions(s - 2, k2)
                turn_x(s + 1, kn)
                project_o(s - 1, k1)
            steps(pe, *SA, body)

            pe.wait_ge(carry_sb, UNITS + 1)
            nc.tensor.matmul(obank[:, 0:E], tri_b[:, 1, :], carry[:], start=True, stop=True).then_inc(cnt_ps, 1)

            def turn_rows(s, k):
                if has(k, 0, TILES):
                    pe.wait_ge(rows_in[s.par], (s.half + 1) * 16)
                    wait(pe, bx_sb, s.n)
                    turn(ps[:, 4, :], lambda t: xl[:, s.par, t, 0:D], ST, bx_ps)

            def hidden(s, k):
                if not has(k, 0, TILES):
                    return
                pe.wait_ge(bx_sb, s.n + 1)
                pe.wait_ge(bw_sb, (s.n + 1) * 2)
                wait(pe, h_sb, (s.n - 1) * 2)
                for f in range(FT):
                    mm = nc.tensor.matmul(ps[:, 2 * s.par + f // 2, (f % 2) * TS:(f % 2 + 1) * TS],
                                          wb1[:, s.par, f, :], xbt[:, s.par], start=True, stop=True)
                    if f % 2:
                        mm.then_inc(h_ps, 1)

            def outputs(s, k):
                if not has(k, 0, TILES):
                    return
                pe.wait_ge(h_sb, (s.n + 1) * 2)
                wait(pe, by_sb, s.n)
                for f in range(FT):
                    mm = nc.tensor.matmul(ps[:, 5, 0:TS], wb2[:, s.par, f, :], hb[:, s.par, f, :],
                                          start=(f == 0), stop=(f == FT - 1))
                mm.then_inc(by_ps, 1)

            def turn_out(s, k):
                if has(k, 0, TILES):
                    pe.wait_ge(by_sb, s.n + 1)
                    wait(pe, yo_sb, s.n * ST)
                    turn(ps[:, 6, :], lambda t: ytb[:, s.par, t * P:(t + 1) * P], ST, yo_ps)

            pe.wait_ge(table_sb, 2)
            turn_rows(Step(0, 0), 0)

            def bodyb(s, k):
                k1, k2, kn = (None,) * 3 if k is None else (k - 1, k - 2, k + 1)
                turn_rows(s + 1, kn)
                hidden(s, k)
                outputs(s - 1, k1)
                turn_out(s - 2, k2)
            steps(pe, *SB, bodyb)

        @block.vector
        def _(dve):
            v = nc.vector
            dve.wait_ge(const_in, 16 * len(CONSTS))
            dve.wait_ge(wg1t_ps, 1)
            v.tensor_copy(wg1t[:], tbank[0:16, 0:P]).then_inc(setup_dve, 1)
            v.tensor_copy(tri_b[:], tri_f[:]).then_inc(setup_dve, 1)
            v.memset(carry[:], 0.0).then_inc(carry_sb, 1)
            for g in range(G):
                v.tensor_copy(wvr[:, g].rearrange("p j h k -> p (j h) k"),
                              wv[:, g].rearrange("p j h -> p (j h)").unsqueeze(2).to_broadcast([P, 2 * H, DK])
                              ).then_inc(setup_dve, 1)
            dve.wait_ge(wdec_ps, 1)
            for j in range(2):
                v.tensor_copy(wdec[:, j], obank[:, 0:HK]).then_inc(setup_dve, 1)
            dve.wait_ge(setup_pool, 7)
            v.tensor_copy(iop[:], iop_i[:]).then_inc(setup_dve, 1)
            v.tensor_copy(iot[:], iot_i[:]).then_inc(setup_dve, 1)
            v.tensor_copy(dest[:], dest_i[:]).then_inc(setup_dve, 1)
            v.memset(eps[:, 0:1], EPS).then_inc(setup_dve, 1)
            v.memset(eps[:, 1:2], DV * EPS).then_inc(setup_dve, 1)

            def log_sigmoid(s, k):
                if has(k, 0, UNITS):
                    dve.wait_ge(dchain, (s.n + 1) * 3)
                    wait(dve, dec_sb, s.n)
                    v.scalar_tensor_tensor(out=dls[:], in0=ring[1], scalar=0.0, in1=dln[:], op0=ALU.min,
                                           op1=ALU.subtract).then_inc(ls_sb, 1)

            def scan(s, k, groups):
                if not has(k, 0, UNITS):
                    return
                for g in groups:
                    if g == 0:
                        dve.wait_ge(k_sb, s.n + 1)
                    dve.wait_ge(v_ps, s.n * G + g + 1)
                    wait(dve, scan_sb, (s.n - 1) * (G * BU) + (g + 1) * BU)
                    v.tensor_tensor(kv[:, g], ring[g], ks[:, s.par], ALU.mult).then_inc(kv_sb, 1)
                for g in groups:
                    dve.wait_ge(kv_sb, s.n * G + g + 1)
                    dve.wait_ge(dec_sb, s.n + 1)
                    wait(dve, qst_sb, (s.n - 2) * G + g + 1 if k is None or k >= 2 else 0)
                    for b in range(BU):
                        a, z = b * L, (b + 1) * L
                        v.tensor_tensor_scan(state[:, s.par, g, a:z], dec[:, s.par, a:z], kv[:, g, a:z], 0.0,
                                             ALU.mult, ALU.add).then_inc(scan_sb, 1)

            def gates(s, k):
                if not has(k, 0, UNITS):
                    return
                dve.wait_ge(ge_sb, s.n + 1)
                v.tensor_scalar(ge1[:], ge[:], 1.0, None, ALU.add).then_inc(gchain, 1)
                dve.wait_ge(gchain, s.n * 2 + 1)
                v.reciprocal(gr[:], ge1[:]).then_inc(gchain, 1)
                dve.wait_ge(gchain, s.n * 2 + 2)
                v.scalar_tensor_tensor(out=gate[:, s.par], in0=ring[3], scalar=bgc[:], in1=gr[:], op0=ALU.add,
                                       op1=ALU.mult).then_inc(gate_sb, 1)

            def head_sum(s, k):
                if has(k, 0, UNITS):
                    dve.wait_ge(osq_sb, s.n + 1)
                    wait(dve, hln_sb, s.n)
                    v.tensor_reduce(hss[:], osq[:].rearrange("p (h e) -> p h e", e=DV), AX.X, ALU.add
                                    ).then_inc(hss_sb, 1)

            def head_apply(s, k):
                if has(k, 0, UNITS):
                    dve.wait_ge(hrs_sb, s.n + 1)
                    wait(dve, on_t, s.n - 1)
                    v.scalar_tensor_tensor(out=on[:, s.par].rearrange("p (h e) -> p h e", e=DV),
                                           in0=obank.rearrange("p (h e) -> p h e", e=DV), scalar=DV ** 0.5,
                                           in1=hrs[:].unsqueeze(2).to_broadcast([P, TL * H, DV]),
                                           op0=ALU.mult, op1=ALU.mult).then_inc(on_sb, 1)

            def apply_gate(s, k):
                if has(k, 0, UNITS):
                    dve.wait_ge(on_t, s.n + 1)
                    dve.wait_ge(gate_sb, s.n + 1)
                    wait(dve, wo_ps, s.n)
                    v.tensor_tensor(go[:], tbank, gate[:, s.par], ALU.mult).then_inc(go_sb, 1)

            def layer_stats(s, k):
                if not has(k, 0, UNITS):
                    return
                dve.wait_ge(wo_ps, s.n + 1)
                dve.wait_ge(xr_in[s.par], (s.half + 1) * 16)
                v.tensor_tensor(rsum[:].rearrange("p t d -> p (t d)"), wbank,
                                xr[:, s.par].rearrange("p t d -> p (t d)"), ALU.add).then_inc(r_sb, 1)
                dve.wait_ge(r_sb, s.n + 1)
                for t in range(TL):
                    v.bn_stats(st6[:, t, :], rsum[:, t, :]).then_inc(lchain, 1)
                dve.wait_ge(lchain, s.n * 8 + TL)
                settle(dve)
                for t in range(TL):
                    v.bn_aggr(mv[:, t, :], st6[:, t, :]).then_inc(lchain, 1)

            def layer_apply(s, k):
                if not has(k, 0, UNITS):
                    return
                dve.wait_ge(lrs_sb, s.n + 1)
                if k is None or k >= 2:
                    dve.wait_ge(scattered[s.par], s.half * (TL * 2 * 16))
                    dve.wait_ge(yres_sb, s.n - 1)
                    dve.wait_ge(y_t, s.n - 1)
                for t in range(TL):
                    v.tensor_scalar(ys[:, s.par, t, 0:D], rsum[:, t, :], mv[:, t, 0:1], lrs[:, t:t + 1],
                                    ALU.subtract, ALU.mult).then_inc(y_sb, 1)

            def choose(s, k):
                if not has(k, 0, UNITS):
                    return
                dve.wait_ge(lg_ps, s.n + 1)
                settle(dve)
                for t in range(TL):
                    v.max(m8[:, t, :], lbank[:, t * E:(t + 1) * E]).then_inc(rchain, 1)
                dve.wait_ge(rchain, s.n * 11 + TL)
                settle(dve)
                for t in range(TL):
                    v.max_index(i8[:, t, :], m8[:, t, :], lbank[:, t * E:(t + 1) * E]).then_inc(rchain, 1)
                wait(dve, we_sb, s.n)
                v.tensor_tensor(wd[:], m8[:, :, 1], m8[:, :, 0], ALU.subtract).then_inc(wd_sb, 1)
                dve.wait_ge(rchain, s.n * 11 + 8)
                v.tensor_copy(idf[:], i8[:, :, 0:2]).then_inc(rchain, 1)
                dve.wait_ge(rchain, s.n * 11 + 9)
                v.tensor_tensor(oneh[:].rearrange("p t c e -> p (t c) e"),
                                iota_e[:, 0:1, :].to_broadcast([P, TL * 2, E]),
                                idf[:].rearrange("p t c -> p (t c)").unsqueeze(2).to_broadcast([P, TL * 2, E]),
                                ALU.is_equal).then_inc(rchain, 1)
                dve.wait_ge(rchain, s.n * 11 + 10)
                wait(dve, pos_ps, s.n)
                v.tensor_tensor(mask[:], oneh[:, :, 0, :], oneh[:, :, 1, :], ALU.add).then_inc(mask_sb, 1)
                dve.wait_ge(mask_sb, s.n + 1)
                v.tensor_reduce(msum[:], mask[:].rearrange("p t e -> p e t"), AX.X, ALU.add).then_inc(rchain, 1)

            def weights(s, k):
                if not has(k, 0, UNITS):
                    return
                dve.wait_ge(we_sb, s.n + 1)
                v.tensor_scalar(we1[:], we[:], 1.0, None, ALU.add).then_inc(wchain, 1)
                dve.wait_ge(wchain, s.n * 3 + 1)
                v.reciprocal(w0[:], we1[:]).then_inc(wchain, 1)
                dve.wait_ge(wchain, s.n * 3 + 2)
                v.tensor_tensor(w1f[:], w0[:], we[:], ALU.mult).then_inc(wchain, 1)
                dve.wait_ge(wchain, s.n * 3 + 3)
                if k is None or k >= 2:
                    dve.wait_ge(scattered[s.par], s.half * (TL * 2 * 16))
                v.tensor_copy(ys[:, s.par, :, F_EXPERT], idf[:, :, 0]).then_inc(field_sb, 1)
                v.tensor_copy(ys[:, s.par, :, F_W1], w1f[:]).then_inc(field_sb, 1)
                v.tensor_tensor(ys[:, s.par, :, F_DW], w0[:], w1f[:], ALU.subtract).then_inc(field_sb, 1)
                v.tensor_copy(ys[:, s.par, :, F_DEST], dest[:, bass.ds(s.n * TL, TL)]).then_inc(dest_sb, 1)

            def slots(s, k):
                if not has(k, 0, UNITS):
                    return
                dve.wait_ge(pos_ps, s.n + 1)
                v.tensor_tensor(sbase[:], pbank.rearrange("p (t e) -> p t e", e=E),
                                iota_e[:, 1:2, :].to_broadcast([P, TL, E]), ALU.add).then_inc(schain, 1)
                dve.wait_ge(rchain, (s.n + 1) * 11)
                v.tensor_tensor(carry[:], carry[:], msum[:], ALU.add).then_inc(carry_sb, 1)
                dve.wait_ge(schain, s.n * 3 + 1)
                for c in range(2):
                    ins = v.tensor_tensor(sprod[:, :, c, :], oneh[:, :, c, :], sbase[:], ALU.mult)
                ins.then_inc(schain, 1)
                dve.wait_ge(schain, s.n * 3 + 2)
                v.tensor_reduce(slotf[:], sprod[:].rearrange("p t c e -> p (t c) e"), AX.X, ALU.add
                                ).then_inc(schain, 1)
                dve.wait_ge(schain, s.n * 3 + 3)
                v.tensor_copy(slot[:, s.par], slotf[:]).then_inc(slot_sb, 1)

            def body(s, k):
                k1, k2 = (None, None) if k is None else (k - 1, k - 2)
                log_sigmoid(s, k)
                layer_apply(s - 2, k2)
                head_sum(s - 1, k1)
                scan(s, k, (0, 1))
                head_apply(s - 1, k1)
                gates(s, k)
                choose(s - 2, k2)
                scan(s, k, (2,))
                apply_gate(s - 1, k1)
                scan(s, k, (3,))
                weights(s - 2, k2)
                slots(s - 2, k2)
                layer_stats(s - 1, k1)
            steps(dve, *SA, body)

            n = [0]

            def link(ins):
                n[0] += 1
                ins.then_inc(tchain, 1)
                dve.wait_ge(tchain, n[0])

            def over_t(a):
                return a.unsqueeze(1).to_broadcast([P, TILES, E])

            def over_e(a):
                return a.unsqueeze(2).to_broadcast([P, TILES, E])

            dve.wait_ge(cnt_ps, 1)
            link(v.tensor_copy(cnt[:], obank[:, 0:E]))
            link(v.tensor_tensor(tbase[:], cnt[:], iota_e[:, 1, :], ALU.add))
            link(v.tensor_scalar(padf[:, 0, :], tbase[:], iop[:], None, ALU.add))
            link(v.tensor_scalar(padf[:, 1, :], padf[:, 0, :], float(P), None, ALU.add))
            v.tensor_copy(padi[:], padf[:]).then_inc(pad_sb, 1)
            link(v.tensor_scalar(cnt[:], cnt[:], float(TS - 1), None, ALU.add))
            link(v.tensor_copy(cnti[:], cnt[:]))
            link(v.tensor_scalar(cnts[:], cnti[:], TS.bit_length() - 1, None, ALU.arith_shift_right))
            link(v.tensor_copy(ntf[:], cnts[:]))
            link(v.tensor_tensor_scan(tend[:], iota_e[:, 2, :], ntf[:], 0.0, ALU.mult, ALU.add))
            link(v.tensor_tensor(tstart[:], tend[:], ntf[:], ALU.subtract))
            link(v.scalar_tensor_tensor(out=tbase[:], in0=tstart[:], scalar=-float(TS), in1=iota_e[:, 1, :],
                                        op0=ALU.mult, op1=ALU.add))
            link(v.tensor_scalar(tbase[:], tbase[:], -float(DUMP), None, ALU.add))
            link(v.tensor_tensor(tge[:], over_e(iot[:]), over_t(tend[:]), ALU.is_ge))
            link(v.tensor_tensor(tgs[:], over_e(iot[:]), over_t(tstart[:]), ALU.is_ge))
            link(v.tensor_tensor(tin[:], tgs[:], tge[:], ALU.subtract))
            link(v.tensor_tensor(tin2[:], tin[:], over_t(tbase[:]), ALU.mult))
            link(v.tensor_reduce(texp[:], tge[:], AX.X, ALU.add))
            link(v.tensor_reduce(tvalid[:], tin[:], AX.X, ALU.add))
            link(v.tensor_reduce(trow[:], tin2[:], AX.X, ALU.add))
            link(v.tensor_scalar(texp[:], texp[:], float(E - 1), None, ALU.min))
            link(v.tensor_tensor(tvalid[:], tvalid[:], iot[:], ALU.mult))
            link(v.scalar_tensor_tensor(out=trow2[:], in0=tvalid[:], scalar=float(TS), in1=trow[:], op0=ALU.mult,
                                        op1=ALU.add))
            link(v.tensor_scalar(trow2[:], trow2[:], float(DUMP), None, ALU.add))
            v.tensor_copy(row_i[:], trow2[:]).then_inc(table_sb, 1)
            v.tensor_copy(exp_i[:], texp[:]).then_inc(table_sb, 1)
            dve.wait_ge(table_sb, 2)
            dve.wait_ge(expert_in, 16 * (1 + E))

            def copy_weights(s, k):
                if not has(k, 0, TILES):
                    return
                e = dve.value_load(exp_i[0:1, bass.ds(s.n, 1)], min_val=0, max_val=E - 1)
                wait(dve, h_ps, (s.n - 1) * 2)
                v.tensor_copy(wb1[:, s.par].rearrange("p f m -> p (f m)"),
                              w1s[:, bass.ds(e, 1), :].rearrange("p a f -> p (a f)")).then_inc(bw_sb, 1)
                wait(dve, by_ps, s.n - 1)
                v.tensor_copy(wb2[:, s.par].rearrange("p f m -> p (f m)"),
                              w2s[:, bass.ds(e, 1), :, :].rearrange("p a f m -> p (a f m)")).then_inc(bw_sb, 1)

            def copy_rows(s, k):
                if has(k, 0, TILES):
                    dve.wait_ge(bx_ps, s.n + 1)
                    wait(dve, h_ps, (s.n - 1) * 2)
                    v.tensor_copy(xbt[:, s.par], ps[:, 4, 0:TS]).then_inc(bx_sb, 1)

            def fields(s, k):
                if not has(k, 0, TILES):
                    return
                dve.wait_ge(rows_in[s.par], (s.half + 1) * 16)
                wait(dve, field_read, s.n)
                v.tensor_scalar(fsel[:], xl[:, s.par, :, F_EXPERT], texp[:, bass.ds(s.n, 1)], None, ALU.is_equal
                                ).then_inc(fchain, 1)
                dve.wait_ge(fchain, s.n * 3 + 1)
                v.tensor_tensor(fwd[:], fsel[:], xl[:, s.par, :, F_DW], ALU.mult).then_inc(fchain, 1)
                dve.wait_ge(fchain, s.n * 3 + 2)
                wait(dve, yo_sb, (s.n - 1) * ST)
                wait(dve, returned[s.par], s.half * (ST * 16))
                v.tensor_tensor(fw[:, s.par], fwd[:], xl[:, s.par, :, F_W1], ALU.add).then_inc(fchain, 1)
                v.scalar_tensor_tensor(out=fdst[:, s.par], in0=fsel[:], scalar=-float(TOKENS),
                                       in1=xl[:, s.par, :, F_DEST], op0=ALU.mult, op1=ALU.add
                                       ).then_inc(field_read, 1)

            def copy_out(s, k):
                if has(k, 0, TILES):
                    dve.wait_ge(by_ps, s.n + 1)
                    wait(dve, yo_ps, s.n - 1)
                    v.tensor_copy(ytb[:, s.par], ps[:, 5, 0:TS]).then_inc(by_sb, 1)

            copy_weights(Step(0, 0), 0)
            copy_rows(Step(0, 0), 0)

            def bodyb(s, k):
                k1, kn = (None, None) if k is None else (k - 1, k + 1)
                copy_rows(s + 1, kn)
                copy_weights(s + 1, kn)
                copy_out(s - 1, k1)
                fields(s, k)
            steps(dve, *SB, bodyb)

            def final_stats(s, k):
                if not has(k, 0, GROUPS):
                    return
                dve.wait_ge(ya_sb, s.n + 1)
                yv = ya[:, s.par]
                v.tensor_tensor(yv, yv, yres[:, bass.ds(s.n * CG, CG), :], ALU.add).then_inc(cchain, 1)
                dve.wait_ge(cchain, s.n * (2 * CG + 1) + 1)
                for t in range(CG):
                    v.bn_stats(cs6[:, t, :], yv[:, t, :]).then_inc(cchain, 1)
                dve.wait_ge(cchain, s.n * (2 * CG + 1) + 1 + CG)
                settle(dve)
                for t in range(CG):
                    v.bn_aggr(cmv[:, s.par, t, :], cs6[:, t, :]).then_inc(cchain, 1)

            def final_apply(s, k):
                if not has(k, 0, GROUPS):
                    return
                dve.wait_ge(crs_sb, s.n + 1)
                wait(dve, stored[s.par], s.half * 16)
                for t in range(CG):
                    v.tensor_scalar(co[:, s.par, t, :], ya[:, s.par, t, :], cmv[:, s.par, t, 0:1],
                                    crs[:, t:t + 1], ALU.subtract, ALU.mult).then_inc(co_sb, 1)

            def bodyc(s, k):
                final_stats(s, k)
                final_apply(s - 1, None if k is None else k - 1)
            steps(dve, *SC, bodyc)


_OUT = (TOKENS, D)


def kernel(L0_attn_inputs, L0_attn_Wq, L0_attn_Wk, L0_attn_Wg1, L0_attn_Wg2, L0_attn_Wv, L0_attn_Wg, L0_attn_bg,
           L0_attn_Wo, L0_ffn_gate_w, L0_ffn_w1, L0_ffn_w2):
    import concourse.bacc as _bacc
    from concourse.bass_utils import run_bass_kernel_spmd as _run

    f32 = np.float32
    arrays = {
        "x": np.ascontiguousarray(np.asarray(L0_attn_inputs).reshape(UNITS, TL, P, D).transpose(0, 2, 1, 3)),
        "Wk": np.ascontiguousarray(L0_attn_Wk),
        "Wq": np.ascontiguousarray(L0_attn_Wq),
        "Wg1": np.ascontiguousarray(L0_attn_Wg1),
        "Wg2": np.ascontiguousarray(L0_attn_Wg2),
        "WvG": np.ascontiguousarray(np.asarray(L0_attn_Wv).reshape(D, H, G, 2).transpose(0, 2, 3, 1)),
        "Wg": np.ascontiguousarray(L0_attn_Wg),
        "bg": np.ascontiguousarray(np.asarray(L0_attn_bg).reshape(D, 1)),
        "Wo": np.ascontiguousarray(L0_attn_Wo),
        "gate_wT": np.ascontiguousarray(np.asarray(L0_ffn_gate_w).T),
        "w1": np.ascontiguousarray(L0_ffn_w1),
        "w2": np.ascontiguousarray(L0_ffn_w2),
    }
    head_of_row = np.tile(np.repeat(np.arange(H), DK), 2)
    j_of_row = np.repeat(np.arange(2), HK)
    head_of_col, dv_of_col = np.repeat(np.arange(H), DV), np.tile(np.arange(DV), H)
    same_head = head_of_row[:, None, None] == head_of_col[None, None, :]
    same_dv = (2 * np.arange(G)[None, :, None] + j_of_row[:, None, None]) == dv_of_col[None, None, :]
    arrays["center"] = (same_head * (same_dv - 1.0 / DV)).astype(f32)
    arrays["ident"] = np.eye(P, dtype=f32)
    arrays["tri"] = np.stack([np.triu(np.ones((P, P), f32), 1), np.ones((P, P), f32)], 1)
    arrays["iota8"] = np.broadcast_to(np.stack([np.arange(E), np.arange(E) * REGION, np.ones(E)]).astype(f32),
                                      (P, 3, E)).copy()
    nc = _bacc.Bacc("TRN2", target_bir_lowering=False, num_devices=1)
    aps = {n: nc.dram_tensor(n, a.shape, mybir.dt.from_np(a.dtype), kind="ExternalInput").ap()
           for n, a in arrays.items()}
    out = nc.dram_tensor("out", _OUT, F32, kind="ExternalOutput").ap()
    build(nc, out=out, **aps)
    r = _run(nc, [arrays], core_ids=[0])
    return r.results[0]["out"].reshape(np.asarray(L0_attn_inputs).shape)
```

```python
from contextlib import ExitStack

import concourse.bass as bass
import numpy as np
from concourse import mybir

F32 = mybir.dt.float32
BF16 = mybir.dt.bfloat16
I32 = mybir.dt.int32
U32 = mybir.dt.uint32
ALU = mybir.AluOpType
ACT = mybir.ActivationFunctionType
AX = mybir.AxisListType

P = 128
D = 128
H, DK, DV = 16, 4, 8
HK = H * DK
NB, L = 32, 256
TOKENS = NB * L
E, F = 8, 512
FT = F // P
EPS = 1e-5
GATE_NORM = 16.0

UNIT = 512
TL = UNIT // P
UNITS = TOKENS // UNIT
BU = UNIT // L
G = 4

TS = 256
ST = TS // P
TILES = (2 * TOKENS - E) // TS + E
REGION = TOKENS + TS
RB = 4
DUMP = E * REGION
ROW = D + 4
F_DEST, F_EXPERT, F_DW, F_W1 = D, D + 1, D + 2, D + 3
NOWHERE = 1.0e6

CG = 8
TT = TOKENS // P
GROUPS = TT // CG


class Step:

    def __init__(self, i, c, m=2):
        self.i, self.c, self.m = i, c, m

    def __add__(self, k):
        return Step(self.i, self.c + k, self.m)

    def __sub__(self, k):
        return Step(self.i, self.c - k, self.m)

    @property
    def n(self):
        return self.i * self.m + self.c

    def of(self, k):
        return self.c % k

    def turns(self, k):
        return self.i * (self.m // k) + self.c // k

    @property
    def par(self):
        return self.of(2)

    @property
    def half(self):
        return self.turns(2)


def wait(eng, sem, value):
    if isinstance(value, int) and value <= 0:
        return
    eng.wait_ge(sem, value)


def steps(eng, first, loop_from, loop_to, last, m, body):
    loop_to -= (loop_to - loop_from) % m
    for s in range(first, loop_from):
        body(Step(s // m, s % m, m), s)
    with eng.Fori(loop_from // m, loop_to // m) as i:
        for c in range(m):
            body(Step(i, c, m), None)
    for s in range(loop_to, last + 1):
        body(Step(s // m, s % m, m), s)


def has(s, k, count):
    return s is None or 0 <= s - k < count


def build(nc, x, Wk, Wq, Wg1, Wg2, WvG, Wg, bg, Wo, gate_wT, w1, w2, ident, center, tri, iota8, out):
    with ExitStack() as ctx:
        def sb(name, shape, dt=F32):
            return ctx.enter_context(nc.sbuf_tensor(name, shape, dt))

        def sem(name):
            return ctx.enter_context(nc.semaphore(name))

        rows = nc.dram_tensor("expert_rows", (DUMP + TS, ROW), F32).ap()
        ybuf = nc.dram_tensor("expert_out", (2 * TOKENS, D), F32).ap()

        ps = ctx.enter_context(nc.psum_tensor("ps", [P, 8, 512], F32))
        kbank, dbank, zbank, qbank = (ps[:, b, :] for b in range(4))
        vbank = (kbank, dbank, qbank, zbank)
        tbank, obank, wbank = ps[:, 4, :], ps[:, 5, :], ps[:, 6, :]
        lbank = ps[:, 7, 0:TL * E]
        pbank = ps[:, 7, 64:64 + TL * E]

        idn = sb("idn", [P, P])
        cen = sb("cen", [P, G, P])
        tri_f = sb("tri_f", [P, 2, P])
        tri_b = sb("tri_b", [P, 2, P], BF16)
        iota_e = sb("iota_e", [P, 3, E])
        wk = sb("wk", [P, 2, HK])
        wq = sb("wq", [P, 2, HK])
        wg1 = sb("wg1", [P, 16])
        wg1t = sb("wg1t", [16, P])
        wg2 = sb("wg2", [16, HK])
        wdec = sb("wdec", [P, 2, HK])
        wv = sb("wv", [P, G, 2, H])
        wvr = sb("wvr", [P, G, 2, H, DK])
        wg = sb("wg", [P, D])
        bgc = sb("bgc", [P, 1])
        nbg = sb("nbg", [P, 1])
        eps = sb("eps", [P, 2])
        wo = sb("wo", [P, D])
        gw = sb("gw", [P, E])
        w1s = sb("w1s", [P, E, F])
        w2s = sb("w2s", [P, E, FT, D])

        xs = sb("xs", [P, 2, TL, D])
        xr = sb("xr", [P, 2, TL, D])
        xt = sb("xt", [P, 2, UNIT])
        ks = sb("ks", [P, 2, UNIT])
        qs = sb("qs", [P, 2, UNIT])
        sabs = sb("sabs", [P, 2, UNIT])
        sexp = sb("sexp", [P, 2, UNIT])
        sln = sb("sln", [P, 2, UNIT])
        sls = sb("sls", [P, 2, UNIT])
        dec = sb("dec", [P, 2, UNIT])
        kv = sb("kv", [P, G, UNIT])
        state = sb("state", [P, 2, G, UNIT])
        qst = sb("qst", [P, 2, G, UNIT])
        gsig = sb("gsig", [P, UNIT])
        gate = sb("gate", [P, 2, UNIT])
        osq = sb("osq", [P, UNIT])
        hss = sb("hss", [P, TL * H])
        hln = sb("hln", [P, TL * H])
        hrs = sb("hrs", [P, TL * H])
        on = sb("on", [P, 2, UNIT])
        go = sb("go", [P, UNIT])
        rsum = sb("rsum", [P, TL, D])
        st6 = sb("st6", [P, TL, 6])
        mv = sb("mv", [P, TL, 2])
        lln = sb("lln", [P, TL])
        lrs = sb("lrs", [P, TL])
        ys = sb("ys", [P, 2, TL, ROW])
        yres = sb("yres", [P, TT, D])
        yt = sb("yt", [P, UNIT])
        m8 = sb("m8", [P, TL, 8])
        i8 = sb("i8", [P, TL, 8], U32)
        idf = sb("idf", [P, TL, 2])
        oneh = sb("oneh", [P, TL, 2, E])
        mask = sb("mask", [P, TL, E], BF16)
        msum = sb("msum", [P, E])
        carry = sb("carry", [P, E], BF16)
        wd = sb("wd", [P, TL])
        we = sb("we", [P, TL])
        we1 = sb("we1", [P, TL])
        w0 = sb("w0", [P, TL])
        w1f = sb("w1f", [P, TL])
        sbase = sb("sbase", [P, TL, E])
        sprod = sb("sprod", [P, TL, 2, E])
        slotf = sb("slotf", [P, TL * 2])
        slot = sb("slot", [P, 2, TL * 2], I32)
        dest_i = sb("dest_i", [P, TT], I32)
        dest = sb("dest", [P, TT])

        padrow = sb("padrow", [P, ROW])
        iop_i = sb("iop_i", [P, 1], I32)
        iop = sb("iop", [P, 1])
        iot_i = sb("iot_i", [P, TILES], I32)
        iot = sb("iot", [P, TILES])
        cnt = sb("cnt", [P, E])
        padf = sb("padf", [P, 2, E])
        padi = sb("padi", [P, 2, E], I32)
        cnti = sb("cnti", [P, E], I32)
        cnts = sb("cnts", [P, E], I32)
        ntf = sb("ntf", [P, E])
        tend = sb("tend", [P, E])
        tstart = sb("tstart", [P, E])
        tbase = sb("tbase", [P, E])
        flat_q = qst[:].rearrange("p u g t -> p (u g t)")
        tge, tgs, tin, tin2 = (
            flat_q[:, k * TILES * E:(k + 1) * TILES * E].rearrange("p (t e) -> p t e", e=E) for k in range(4))
        texp = sb("texp", [P, TILES])
        tvalid = sb("tvalid", [P, TILES])
        trow = sb("trow", [P, TILES])
        trow2 = sb("trow2", [P, TILES])
        row_i = sb("row_i", [P, TILES], I32)
        exp_i = sb("exp_i", [P, TILES], I32)

        xl = sb("xl", [P, RB, ST, ROW])
        xbt = sb("xbt", [P, 2, TS])
        wb1 = state[:, 0].rearrange("p (u a) (f m) -> p u (a f) m", u=2, f=4)[:, :, 0:FT, :]
        wb2 = state[:, 1].rearrange("p (u a) (f m) -> p u (a f) m", u=2, f=4)[:, :, 0:FT, :]
        hb = kv[:].rearrange("p (u a) (f t) -> p u (a f) t", u=2, f=2)
        ytb = sb("ytb", [P, 2, TS])
        yo = sb("yo", [P, RB, ST, D])
        fsel = sb("fsel", [P, ST])
        fwd = sb("fwd", [P, ST])
        fw = sb("fw", [P, RB, ST])
        fdst = sb("fdst", [P, RB, ST], I32)

        def reuse(buf, k):
            return buf[:, k].rearrange("p g (a t d) -> p (g a) t d", a=1, d=D).rearrange(
                "p (u g) t d -> p u (g t) d", u=2)

        y0, y1, ya, co = reuse(state, 0), reuse(state, 1), reuse(qst, 0), reuse(qst, 1)
        cs6 = sb("cs6", [P, CG, 6])
        cmv = sb("cmv", [P, 2, CG, 2])
        cln = sb("cln", [P, CG])
        crs = sb("crs", [P, CG])

        const_in = sem("const_in")
        expert_in = sem("expert_in")
        dump_in = sem("dump_in")
        x_in = [sem("x_in0"), sem("x_in1")]
        xr_in = [sem("xr_in0"), sem("xr_in1")]
        setup_pool = sem("setup_pool")
        setup_dve = sem("setup_dve")
        nbg_sb = sem("nbg_sb")
        pool_passed, dve_passed = sem("pool_passed"), sem("dve_passed")
        wg1t_ps = sem("wg1t_ps")
        wdec_ps = sem("wdec_ps")
        xt_ps, xt_sb = sem("xt_ps"), sem("xt_sb")
        k_ps, d_ps, q_ps, z_ps, v_ps = (sem(s) for s in ("k_ps", "d_ps", "q_ps", "z_ps", "v_ps"))
        k_sb, q_sb = sem("k_sb"), sem("q_sb")
        sabs_sb, sexp_sb, sln_sb, sls_sb, dec_sb, gsig_sb, gate_sb = (
            sem(s) for s in ("sabs_sb", "sexp_sb", "sln_sb", "sls_sb", "dec_sb", "gsig_sb", "gate_sb"))
        kv_sb, scan_sb, qst_sb = sem("kv_sb"), sem("scan_sb"), sem("qst_sb")
        o_ps, osq_sb, hss_sb, hln_sb, hrs_sb, on_sb = (
            sem(s) for s in ("o_ps", "osq_sb", "hss_sb", "hln_sb", "hrs_sb", "on_sb"))
        on_t, go_sb, wo_ps = sem("on_t"), sem("go_sb"), sem("wo_ps")
        r_sb, lchain, lln_sb, lrs_sb, y_sb = (sem(s) for s in ("r_sb", "lchain", "lln_sb", "lrs_sb", "y_sb"))
        y_t, yt_sb, lg_ps, yres_sb = sem("y_t"), sem("yt_sb"), sem("lg_ps"), sem("yres_sb")
        rchain, mask_sb, wd_sb, we_sb, wchain = (
            sem(s) for s in ("rchain", "mask_sb", "wd_sb", "we_sb", "wchain"))
        carry_sb, pos_ps, schain, slot_sb, field_sb, dest_sb = (
            sem(s) for s in ("carry_sb", "pos_ps", "schain", "slot_sb", "field_sb", "dest_sb"))
        scattered = [sem("scattered0"), sem("scattered1")]
        cnt_ps, tchain, pad_sb, table_sb, padded = (
            sem(s) for s in ("cnt_ps", "tchain", "pad_sb", "table_sb", "padded"))
        rows_in = [sem(f"rows_in{k}") for k in range(RB)]
        bx_ps, bx_sb, bw_sb = sem("bx_ps"), sem("bx_sb"), sem("bw_sb")
        h_ps, h_sb, by_ps, by_sb, yo_ps, yo_sb = (
            sem(s) for s in ("h_ps", "h_sb", "by_ps", "by_sb", "yo_ps", "yo_sb"))
        fchain, field_read = sem("fchain"), sem("field_read")
        returned = [sem(f"returned{k}") for k in range(RB)]
        y_in = [sem("y_in0"), sem("y_in1")]
        ya_sb, cchain, cln_sb, crs_sb, co_sb = (sem(s) for s in ("ya_sb", "cchain", "cln_sb", "crs_sb", "co_sb"))
        stored = [sem("stored0"), sem("stored1")]

        CONSTS = [(idn[:], ident), (cen[:], center), (tri_f[:], tri), (iota_e[:], iota8),
                  (wk[:, 0, :], Wk), (wk[:, 1, :], Wk), (wq[:, 0, :], Wq), (wq[:, 1, :], Wq),
                  (wg1[:], Wg1), (wg2[:], Wg2), (wv[:], WvG), (wg[:], Wg), (bgc[:], bg),
                  (wo[:], Wo), (gw[:], gate_wT)]
        SA = (0, 4, UNITS - 2, UNITS + 1, 2)
        SB = (0, 4, TILES - 1, TILES + 1, RB)
        SC = (0, 4, GROUPS, GROUPS, 2)

        block = ctx.enter_context(nc.Block())

        def settle(eng):
            eng.sem_inc(pool_passed if eng is nc.gpsimd else dve_passed, 1)

        @block.sync
        def _(sp):
            def load_x(s, k):
                if not has(k, 0, UNITS):
                    return
                wait(sp, xt_ps, s.n - 1)
                sp.dma_start(xs[:, s.par], x[bass.ds(s.n, 1)].rearrange("u p t d -> (u p) t d")
                             ).then_inc(x_in[s.par], 16)

            def load_xr(s, k):
                if not has(k, 0, UNITS):
                    return
                wait(sp, r_sb, s.n - 1)
                sp.dma_start(xr[:, s.par], x[bass.ds(s.n, 1)].rearrange("u p t d -> (u p) t d")
                             ).then_inc(xr_in[s.par], 16)

            load_x(Step(0, 0), 0)
            for dst, src in CONSTS:
                sp.dma_start(dst, src).then_inc(const_in, 16)
            load_x(Step(0, 1), 1)
            load_xr(Step(0, 0), 0)
            load_xr(Step(0, 1), 1)
            sp.dma_start(w1s[:], w1.rearrange("e d f -> d e f")).then_inc(expert_in, 16)
            for e in range(E):
                sp.dma_start(w2s[:, e], w2[e].rearrange("(t p) d -> p t d", p=P)).then_inc(expert_in, 16)
            sp.wait_ge(setup_pool, 4)
            for k in range(ST):
                sp.dma_start(rows[DUMP + k * P:DUMP + (k + 1) * P, :], padrow[:]).then_inc(dump_in, 16)

            def body(s, k):
                load_x(s, k)
                load_xr(s, k)
            steps(sp, 2, 2, UNITS, UNITS - 1, 2, body)

            for q in scattered:
                sp.wait_ge(q, UNITS // 2 * TL * 2 * 16)
            sp.wait_ge(padded, 16 * ST * E)
            sp.wait_ge(dump_in, 16 * ST)
            sp.wait_ge(table_sb, 2)

            def load_rows(s, k):
                if not has(k, 0, TILES):
                    return
                wait(sp, bx_ps, s.n - RB + 1)
                wait(sp, field_read, s.n - RB + 1)
                at = sp.value_load(row_i[0:1, bass.ds(s.n, 1)], min_val=0, max_val=DUMP)
                sp.dma_start(xl[:, s.of(RB)], rows[bass.ds(at, TS), :].rearrange("(t p) d -> p t d", p=P)
                             ).then_inc(rows_in[s.of(RB)], 16)
            steps(sp, 0, 4, TILES, TILES - 1, RB, load_rows)

            for r, q in enumerate(returned):
                sp.wait_ge(q, len(range(r, TILES, RB)) * ST * 16)
            yv = ybuf.rearrange("(c p t) d -> c p (t d)", c=2, p=P)
            ov = out.rearrange("(t p) d -> p t d", p=P)

            def load_y(s, k):
                if has(k, 0, GROUPS):
                    wait(sp, ya_sb, s.n - 1)
                    for c, buf in enumerate((y0, y1)):
                        sp.dma_start(buf[:, s.par].rearrange("p t d -> p (t d)"),
                                     yv[c, :, bass.ds(s.n * (CG * D), CG * D)]).then_inc(y_in[s.par], 16)

            steps(sp, 0, 2, GROUPS, GROUPS - 1, 2, load_y)

        @block.gpsimd
        def _(pool):
            nc.gpsimd.memset(padrow[:, 0:D], 0.0).then_inc(setup_pool, 1)
            nc.gpsimd.memset(padrow[:, D:ROW], 0.0).then_inc(setup_pool, 1)
            pool.wait_ge(setup_pool, 2)
            nc.gpsimd.memset(padrow[:, F_DEST:F_DEST + 1], NOWHERE).then_inc(setup_pool, 1)
            nc.gpsimd.memset(padrow[:, F_EXPERT:F_EXPERT + 1], -1.0).then_inc(setup_pool, 1)
            nc.gpsimd.iota(iop_i[:], [[0, 1]], base=0, channel_multiplier=1).then_inc(setup_pool, 1)
            nc.gpsimd.iota(iot_i[:], [[1, TILES]], base=0, channel_multiplier=0).then_inc(setup_pool, 1)
            nc.gpsimd.iota(dest_i[:], [[1, TT]], base=TOKENS, channel_multiplier=TT).then_inc(setup_pool, 1)

            def products(s, k):
                if not has(k, 0, UNITS):
                    return
                pool.wait_ge(q_sb, s.n + 1)
                for g in range(G):
                    pool.wait_ge(scan_sb, s.n * (G * BU) + (g + 1) * BU)
                    if g == 0:
                        wait(pool, o_ps, s.n - 1)
                    nc.gpsimd.tensor_tensor(qst[:, s.par, g], qs[:, s.par], state[:, s.par, g],
                                            ALU.mult).then_inc(qst_sb, 1)

            def scatter(s, k):
                if not has(k, 0, UNITS):
                    return
                pool.wait_ge(y_sb, (s.n + 1) * TL)
                pool.wait_ge(field_sb, (s.n + 1) * 3)
                pool.wait_ge(dest_sb, s.n + 1)
                pool.wait_ge(slot_sb, s.n + 1)
                settle(pool)
                for t in range(TL):
                    for c in range(2):
                        m = 2 * t + c
                        pool.indirect_dma_start(
                            out=rows, out_offset=bass.IndirectOffsetOnAxis(ap=slot[:, s.par, m:m + 1], axis=0),
                            in_=ys[:, s.par, t, :], in_offset=None).then_inc(scattered[s.par], 16)

            def body(s, k):
                products(s, k)
                scatter(s - 2, None if k is None else k - 2)
            steps(pool, *SA, body)

            pool.wait_ge(pad_sb, 1)
            for c in range(ST):
                for e in range(E):
                    pool.indirect_dma_start(
                        out=rows, out_offset=bass.IndirectOffsetOnAxis(ap=padi[:, c, e:e + 1], axis=0),
                        in_=padrow[:], in_offset=None).then_inc(padded, 16)

            def give_back(s, k):
                if not has(k, 2, TILES):
                    return
                s = s - 2
                pool.wait_ge(yo_sb, (s.n + 1) * ST)
                settle(pool)
                for t in range(ST):
                    pool.indirect_dma_start(
                        out=ybuf, out_offset=bass.IndirectOffsetOnAxis(ap=fdst[:, s.of(RB), t:t + 1], axis=0),
                        in_=yo[:, s.of(RB), t, :], in_offset=None, bounds_check=2 * TOKENS - 1,
                        oob_is_err=False).then_inc(returned[s.of(RB)], 16)
            steps(pool, *SB, give_back)

            def add_up(s, k):
                if not has(k, 0, GROUPS):
                    return
                pool.wait_ge(y_in[s.par], (s.half + 1) * 32)
                wait(pool, co_sb, (s.n - 1) * CG)
                nc.gpsimd.tensor_tensor(ya[:, s.par], y0[:, s.par], y1[:, s.par], ALU.add).then_inc(ya_sb, 1)
            steps(pool, *SC, add_up)

        @block.scalar
        def _(act):
            nc.scalar.preload_act_table_set("natural_log_exp_and_others")
            act.wait_ge(const_in, 16 * len(CONSTS))
            nc.scalar.activation(nbg[:], bgc[:], ACT.Copy, scale=-1.0).then_inc(nbg_sb, 1)
            act.wait_ge(nbg_sb, 1)
            act.wait_ge(setup_dve, 9 + G)

            def copy_xt(s, k):
                if has(k, 0, UNITS):
                    act.wait_ge(xt_ps, s.n + 1)
                    wait(act, v_ps, (s.n - 1) * G)
                    nc.scalar.activation(xt[:, s.par], tbank, ACT.Copy).then_inc(xt_sb, 1)

            def softplus(s, k):
                if not has(k, 0, UNITS):
                    return
                act.wait_ge(d_ps, s.n + 1)
                wait(act, sexp_sb, s.n)
                nc.scalar.activation(sabs[:, 0], dbank, ACT.Abs).then_inc(sabs_sb, 1)
                act.wait_ge(z_ps, s.n + 1)
                nc.scalar.activation(sabs[:, 1], zbank, ACT.Abs, bias=bgc[:]).then_inc(sabs_sb, 1)
                act.wait_ge(sabs_sb, s.n * 2 + 2)
                wait(act, sln_sb, s.n)
                nc.scalar.activation(sexp[:], sabs[:], ACT.Exp, scale=-1.0).then_inc(sexp_sb, 1)
                act.wait_ge(sexp_sb, s.n + 1)
                wait(act, sls_sb, s.n * 2)
                nc.scalar.activation(sln[:], sexp[:], ACT.Ln, bias=1.0).then_inc(sln_sb, 1)

            def copy_k(s, k):
                if has(k, 0, UNITS):
                    act.wait_ge(k_ps, s.n + 1)
                    wait(act, kv_sb, (s.n - 1) * G)
                    nc.scalar.activation(ks[:, s.par], kbank, ACT.Copy, scale=DK ** -0.5).then_inc(k_sb, 1)

            def sigmoids(s, k):
                if not has(k, 0, UNITS):
                    return
                act.wait_ge(sls_sb, s.n * 2 + 1)
                wait(act, scan_sb, (s.n - 1) * (G * BU))
                nc.scalar.activation(dec[:, s.par], sls[:, 0], ACT.Exp, scale=1.0 / GATE_NORM).then_inc(dec_sb, 1)
                act.wait_ge(sls_sb, s.n * 2 + 2)
                wait(act, gate_sb, s.n)
                nc.scalar.activation(gsig[:], sls[:, 1], ACT.Exp, bias=bgc[:]).then_inc(gsig_sb, 1)

            def copy_q(s, k):
                if has(k, 0, UNITS):
                    act.wait_ge(q_ps, s.n + 1)
                    wait(act, qst_sb, (s.n - 1) * G)
                    nc.scalar.activation(qs[:, s.par], qbank, ACT.Copy).then_inc(q_sb, 1)

            def square(s, k):
                if has(k, 0, UNITS):
                    act.wait_ge(o_ps, s.n + 1)
                    wait(act, on_sb, s.n)
                    nc.scalar.activation(osq[:], obank, ACT.Square).then_inc(osq_sb, 1)

            def root(src, tmp, dst, bias, tmp_sb, dst_sb, n):
                nc.scalar.activation(tmp, src, ACT.Ln, bias=bias).then_inc(tmp_sb, 1)
                act.wait_ge(tmp_sb, n + 1)
                nc.scalar.activation(dst, tmp, ACT.Exp, scale=-0.5).then_inc(dst_sb, 1)

            def head_root(s, k):
                if has(k, 0, UNITS):
                    act.wait_ge(hss_sb, s.n + 1)
                    wait(act, on_sb, s.n)
                    root(hss[:], hln[:], hrs[:], eps[:, 1:2], hln_sb, hrs_sb, s.n)

            def layer_root(s, k):
                if has(k, 0, UNITS):
                    act.wait_ge(lchain, (s.n + 1) * 8)
                    wait(act, y_sb, s.n * TL)
                    root(mv[:, :, 1], lln[:], lrs[:], eps[:, 0:1], lln_sb, lrs_sb, s.n)

            def copy_yt(s, k):
                if has(k, 0, UNITS):
                    act.wait_ge(y_t, s.n + 1)
                    wait(act, lg_ps, s.n)
                    nc.scalar.activation(yt[:], tbank, ACT.Copy).then_inc(yt_sb, 1)

            def keep_y(s, k):
                if has(k, 0, UNITS):
                    act.wait_ge(y_sb, (s.n + 1) * TL)
                    nc.scalar.activation(yres[:, bass.ds(s.n * TL, TL), :], ys[:, s.par, :, 0:D],
                                         ACT.Copy).then_inc(yres_sb, 1)

            def weight_exp(s, k):
                if has(k, 0, UNITS):
                    act.wait_ge(wd_sb, s.n + 1)
                    wait(act, field_sb, s.n * 3)
                    nc.scalar.activation(we[:], wd[:], ACT.Exp).then_inc(we_sb, 1)

            for stage in (copy_xt, softplus, copy_k, copy_q):
                stage(Step(0, 0), 0)

            def body(s, k):
                k1, k2, kn = (None,) * 3 if k is None else (k - 1, k - 2, k + 1)
                sigmoids(s, k)
                copy_yt(s - 2, k2)
                head_root(s - 1, k1)
                copy_xt(s + 1, kn)
                keep_y(s - 2, k2)
                copy_k(s + 1, kn)
                weight_exp(s - 2, k2)
                copy_q(s + 1, kn)
                softplus(s + 1, kn)
                layer_root(s - 1, k1)
                square(s, k)
            steps(act, *SA, body)

            def silu(s, k):
                if not has(k, 0, TILES):
                    return
                for b in range(2):
                    act.wait_ge(h_ps, s.n * 2 + b + 1)
                    if b == 0:
                        wait(act, by_ps, s.n - 1)
                    nc.scalar.activation(hb[:, s.par, 2 * b:2 * b + 2, :].rearrange("p f t -> p (f t)"),
                                         ps[:, 2 * s.par + b, :], ACT.Silu).then_inc(h_sb, 1)

            def weigh(s, k):
                if not has(k, 0, TILES):
                    return
                act.wait_ge(yo_ps, s.n + 1)
                act.wait_ge(fchain, (s.n + 1) * 3)
                act.wait_ge(field_read, s.n + 1)
                wait(act, returned[s.of(RB)], s.turns(RB) * (ST * 16))
                for t in range(ST):
                    nc.scalar.activation(yo[:, s.of(RB), t, :], ps[:, 6, t * D:(t + 1) * D], ACT.Copy,
                                         scale=fw[:, s.of(RB), t:t + 1]).then_inc(yo_sb, 1)

            def bodyb(s, k):
                silu(s, k)
                weigh(s - 2, None if k is None else k - 2)
            steps(act, *SB, bodyb)

            ov = out.rearrange("(t p) d -> p t d", p=P)

            def final_root(s, k):
                if has(k, 0, GROUPS):
                    act.wait_ge(cchain, (s.n + 1) * (2 * CG + 1))
                    wait(act, co_sb, s.n * CG)
                    root(cmv[:, s.par, :, 1], cln[:], crs[:], eps[:, 0:1], cln_sb, crs_sb, s.n)

            def store(s, k):
                if has(k, 0, GROUPS):
                    act.wait_ge(co_sb, (s.n + 1) * CG)
                    act.dma_start(ov[:, bass.ds(s.n * CG, CG), :], co[:, s.par]).then_inc(stored[s.par], 16)

            def bodyc(s, k):
                final_root(s, k)
                store(s - 1, None if k is None else k - 1)
            steps(act, *SC, bodyc)
            for q in stored:
                act.wait_ge(q, GROUPS // 2 * 16)

        @block.tensor
        def _(pe):
            pe.wait_ge(const_in, 16 * len(CONSTS))

            def turn(bank, src, tiles, done):
                for t in range(tiles):
                    mm = nc.tensor.transpose(bank[:, t * P:(t + 1) * P], src(t), idn[:])
                mm.then_inc(done, 1)

            def turn_x(s, k):
                if has(k, 0, UNITS):
                    pe.wait_ge(x_in[s.par], (s.half + 1) * 16)
                    wait(pe, yt_sb, s.n - 2)
                    turn(tbank, lambda t: xs[:, s.par, t, :], TL, xt_ps)

            def project(s, bank, w, done):
                nc.tensor.matmul(bank, w, xt[:, s.par], start=True, stop=True).then_inc(done, 1)

            def flat(w):
                return w.rearrange("p a b -> p (a b)")

            def keys(s, k):
                if has(k, 0, UNITS):
                    pe.wait_ge(xt_sb, s.n + 1)
                    wait(pe, kv_sb, (s.n - 1) * G + 1)
                    project(s, kbank, flat(wk[:]), k_ps)

            def decays(s, k):
                if has(k, 0, UNITS):
                    wait(pe, kv_sb, (s.n - 1) * G + 2)
                    project(s, dbank, flat(wdec[:]), d_ps)

            def queries(s, k):
                if has(k, 0, UNITS):
                    wait(pe, kv_sb, (s.n - 1) * G + 3)
                    project(s, qbank, flat(wq[:]), q_ps)

            def gate_inputs(s, k):
                if has(k, 0, UNITS):
                    wait(pe, kv_sb, s.n * G)
                    project(s, zbank, wg[:], z_ps)

            def values(s, k, g):
                if has(k, 0, UNITS):
                    free = (k_sb, sls_sb, q_sb, gate_sb)[g]
                    pe.wait_ge(free, s.n * 2 + 1 if g == 1 else s.n + 1)
                    project(s, vbank[g], wvr[:, g].rearrange("p j h k -> p (j h k)"), v_ps)

            def heads(s, k):
                if not has(k, 0, UNITS):
                    return
                pe.wait_ge(qst_sb, (s.n + 1) * G)
                wait(pe, on_sb, s.n)
                for t in range(TL):
                    for g in range(G):
                        mm = nc.tensor.matmul(obank[:, t * P:(t + 1) * P], qst[:, s.par, g, t * P:(t + 1) * P],
                                              cen[:, g, :], start=(g == 0), stop=(g == G - 1))
                mm.then_inc(o_ps, 1)

            def turn_o(s, k):
                if has(k, 0, UNITS):
                    pe.wait_ge(on_sb, s.n + 1)
                    wait(pe, yt_sb, s.n)
                    wait(pe, xt_sb, s.n + 3 if k is None else min(s.n + 3, UNITS))
                    turn(tbank, lambda t: on[:, s.par, t * P:(t + 1) * P], TL, on_t)

            def project_o(s, k):
                if not has(k, 0, UNITS):
                    return
                pe.wait_ge(go_sb, s.n + 1)
                wait(pe, r_sb, s.n)
                for t in range(TL):
                    mm = nc.tensor.matmul(wbank[:, t * P:(t + 1) * P], go[:, t * P:(t + 1) * P], wo[:],
                                          start=True, stop=True)
                mm.then_inc(wo_ps, 1)

            def turn_y(s, k):
                if has(k, 0, UNITS):
                    pe.wait_ge(y_sb, (s.n + 1) * TL)
                    pe.wait_ge(go_sb, s.n + 1)
                    turn(tbank, lambda t: ys[:, s.par, t, 0:D], TL, y_t)

            def logits(s, k):
                if not has(k, 0, UNITS):
                    return
                pe.wait_ge(yt_sb, s.n + 1)
                wait(pe, schain, s.n * 3)
                for t in range(TL):
                    mm = nc.tensor.matmul(lbank[:, t * E:(t + 1) * E], yt[:, t * P:(t + 1) * P], gw[:],
                                          start=True, stop=True)
                mm.then_inc(lg_ps, 1)

            def positions(s, k):
                if not has(k, 0, UNITS):
                    return
                pe.wait_ge(mask_sb, s.n + 1)
                wait(pe, carry_sb, s.n + 1)
                m = mask[:].rearrange("p t e -> p (t e)")
                nc.tensor.matmul(pbank, tri_b[:, 0, :], m, start=True, stop=False)
                for t in range(1, TL):
                    nc.tensor.matmul(pbank[:, t * E:], tri_b[:, 1, :], m[:, 0:(TL - t) * E],
                                     start=False, stop=False)
                for t in range(TL):
                    mm = nc.tensor.matmul(pbank[:, t * E:(t + 1) * E], tri_b[:, 1, :], carry[:],
                                          start=False, stop=(t == TL - 1))
                mm.then_inc(pos_ps, 1)

            nc.tensor.transpose(tbank[0:16, 0:P], wg1[:], idn[:]).then_inc(wg1t_ps, 1)
            pe.wait_ge(setup_dve, 1)
            nc.tensor.matmul(obank[:, 0:HK], wg1t[:], wg2[:], start=True, stop=True).then_inc(wdec_ps, 1)
            turn_x(Step(0, 0), 0)
            pe.wait_ge(setup_dve, 9 + G)
            for stage in (keys, decays, queries, gate_inputs):
                stage(Step(0, 0), 0)

            def body(s, k):
                k1, k2, kn = (None,) * 3 if k is None else (k - 1, k - 2, k + 1)
                values(s, k, 0)
                values(s, k, 1)
                turn_y(s - 2, k2)
                values(s, k, 2)
                values(s, k, 3)
                turn_x(s + 1, kn)
                logits(s - 2, k2)
                turn_o(s - 1, k1)
                keys(s + 1, kn)
                decays(s + 1, kn)
                positions(s - 2, k2)
                queries(s + 1, kn)
                project_o(s - 1, k1)
                gate_inputs(s + 1, kn)
                heads(s, k)
            steps(pe, *SA, body)

            pe.wait_ge(carry_sb, UNITS + 1)
            nc.tensor.matmul(obank[:, 0:E], tri_b[:, 1, :], carry[:], start=True, stop=True).then_inc(cnt_ps, 1)

            def turn_rows(s, k):
                if has(k, 0, TILES):
                    pe.wait_ge(rows_in[s.of(RB)], (s.turns(RB) + 1) * 16)
                    wait(pe, bx_sb, s.n)
                    turn(ps[:, 4, :], lambda t: xl[:, s.of(RB), t, 0:D], ST, bx_ps)

            def hidden(s, k):
                if not has(k, 0, TILES):
                    return
                pe.wait_ge(bx_sb, s.n + 1)
                pe.wait_ge(bw_sb, (s.n + 1) * 2)
                wait(pe, h_sb, (s.n - 1) * 2)
                for f in range(FT):
                    mm = nc.tensor.matmul(ps[:, 2 * s.par + f // 2, (f % 2) * TS:(f % 2 + 1) * TS],
                                          wb1[:, s.par, f, :], xbt[:, s.par], start=True, stop=True)
                    if f % 2:
                        mm.then_inc(h_ps, 1)

            def outputs(s, k):
                if not has(k, 0, TILES):
                    return
                pe.wait_ge(h_sb, (s.n + 1) * 2)
                wait(pe, by_sb, s.n)
                for f in range(FT):
                    mm = nc.tensor.matmul(ps[:, 5, 0:TS], wb2[:, s.par, f, :], hb[:, s.par, f, :],
                                          start=(f == 0), stop=(f == FT - 1))
                mm.then_inc(by_ps, 1)

            def turn_out(s, k):
                if has(k, 0, TILES):
                    pe.wait_ge(by_sb, s.n + 1)
                    wait(pe, yo_sb, s.n * ST)
                    turn(ps[:, 6, :], lambda t: ytb[:, s.par, t * P:(t + 1) * P], ST, yo_ps)

            pe.wait_ge(table_sb, 2)
            turn_rows(Step(0, 0, RB), 0)

            def bodyb(s, k):
                k1, k2, kn = (None,) * 3 if k is None else (k - 1, k - 2, k + 1)
                turn_rows(s + 1, kn)
                hidden(s, k)
                outputs(s - 1, k1)
                turn_out(s - 2, k2)
            steps(pe, *SB, bodyb)

        @block.vector
        def _(dve):
            v = nc.vector
            dve.wait_ge(const_in, 16 * len(CONSTS))
            dve.wait_ge(nbg_sb, 1)
            dve.wait_ge(wg1t_ps, 1)
            v.tensor_copy(wg1t[:], tbank[0:16, 0:P]).then_inc(setup_dve, 1)
            v.tensor_copy(tri_b[:], tri_f[:]).then_inc(setup_dve, 1)
            v.memset(carry[:], 0.0).then_inc(carry_sb, 1)
            for g in range(G):
                v.tensor_copy(wvr[:, g].rearrange("p j h k -> p (j h) k"),
                              wv[:, g].rearrange("p j h -> p (j h)").unsqueeze(2).to_broadcast([P, 2 * H, DK])
                              ).then_inc(setup_dve, 1)
            dve.wait_ge(wdec_ps, 1)
            for j in range(2):
                v.tensor_copy(wdec[:, j], obank[:, 0:HK]).then_inc(setup_dve, 1)
            dve.wait_ge(setup_pool, 7)
            v.tensor_copy(iop[:], iop_i[:]).then_inc(setup_dve, 1)
            v.tensor_copy(iot[:], iot_i[:]).then_inc(setup_dve, 1)
            v.tensor_copy(dest[:], dest_i[:]).then_inc(setup_dve, 1)
            v.memset(eps[:, 0:1], EPS).then_inc(setup_dve, 1)
            v.memset(eps[:, 1:2], DV * EPS).then_inc(setup_dve, 1)

            def log_sigmoids(s, k):
                if not has(k, 0, UNITS):
                    return
                dve.wait_ge(sln_sb, s.n + 1)
                wait(dve, dec_sb, s.n)
                v.scalar_tensor_tensor(out=sls[:, 0], in0=dbank, scalar=0.0, in1=sln[:, 0], op0=ALU.min,
                                       op1=ALU.subtract).then_inc(sls_sb, 1)
                wait(dve, gsig_sb, s.n)
                v.scalar_tensor_tensor(out=sls[:, 1], in0=zbank, scalar=nbg[:], in1=sln[:, 1], op0=ALU.min,
                                       op1=ALU.subtract).then_inc(sls_sb, 1)

            def scan(s, k, groups):
                if not has(k, 0, UNITS):
                    return
                for g in groups:
                    if g == 0:
                        dve.wait_ge(k_sb, s.n + 1)
                    dve.wait_ge(v_ps, s.n * G + g + 1)
                    wait(dve, scan_sb, (s.n - 1) * (G * BU) + (g + 1) * BU)
                    v.tensor_tensor(kv[:, g], vbank[g], ks[:, s.par], ALU.mult).then_inc(kv_sb, 1)
                for g in groups:
                    dve.wait_ge(kv_sb, s.n * G + g + 1)
                    dve.wait_ge(dec_sb, s.n + 1)
                    wait(dve, qst_sb, (s.n - 2) * G + g + 1 if k is None or k >= 2 else 0)
                    for b in range(BU):
                        a, z = b * L, (b + 1) * L
                        v.tensor_tensor_scan(state[:, s.par, g, a:z], dec[:, s.par, a:z], kv[:, g, a:z], 0.0,
                                             ALU.mult, ALU.add).then_inc(scan_sb, 1)

            def gates(s, k):
                if not has(k, 0, UNITS):
                    return
                dve.wait_ge(gsig_sb, s.n + 1)
                v.scalar_tensor_tensor(out=gate[:, s.par], in0=zbank, scalar=bgc[:], in1=gsig[:], op0=ALU.add,
                                       op1=ALU.mult).then_inc(gate_sb, 1)

            def head_sum(s, k):
                if has(k, 0, UNITS):
                    dve.wait_ge(osq_sb, s.n + 1)
                    wait(dve, hln_sb, s.n)
                    v.tensor_reduce(hss[:], osq[:].rearrange("p (h e) -> p h e", e=DV), AX.X, ALU.add
                                    ).then_inc(hss_sb, 1)

            def head_apply(s, k):
                if has(k, 0, UNITS):
                    dve.wait_ge(hrs_sb, s.n + 1)
                    wait(dve, on_t, s.n - 1)
                    v.scalar_tensor_tensor(out=on[:, s.par].rearrange("p (h e) -> p h e", e=DV),
                                           in0=obank.rearrange("p (h e) -> p h e", e=DV), scalar=DV ** 0.5,
                                           in1=hrs[:].unsqueeze(2).to_broadcast([P, TL * H, DV]),
                                           op0=ALU.mult, op1=ALU.mult).then_inc(on_sb, 1)

            def apply_gate(s, k):
                if has(k, 0, UNITS):
                    dve.wait_ge(on_t, s.n + 1)
                    dve.wait_ge(gate_sb, s.n + 1)
                    wait(dve, wo_ps, s.n)
                    v.tensor_tensor(go[:], tbank, gate[:, s.par], ALU.mult).then_inc(go_sb, 1)

            def layer_stats(s, k):
                if not has(k, 0, UNITS):
                    return
                dve.wait_ge(wo_ps, s.n + 1)
                dve.wait_ge(xr_in[s.par], (s.half + 1) * 16)
                v.tensor_tensor(rsum[:].rearrange("p t d -> p (t d)"), wbank,
                                xr[:, s.par].rearrange("p t d -> p (t d)"), ALU.add).then_inc(r_sb, 1)
                dve.wait_ge(r_sb, s.n + 1)
                for t in range(TL):
                    v.bn_stats(st6[:, t, :], rsum[:, t, :]).then_inc(lchain, 1)
                dve.wait_ge(lchain, s.n * 8 + TL)
                settle(dve)
                for t in range(TL):
                    v.bn_aggr(mv[:, t, :], st6[:, t, :]).then_inc(lchain, 1)

            def layer_apply(s, k):
                if not has(k, 0, UNITS):
                    return
                dve.wait_ge(lrs_sb, s.n + 1)
                if k is None or k >= 2:
                    dve.wait_ge(scattered[s.par], s.half * (TL * 2 * 16))
                    dve.wait_ge(yres_sb, s.n - 1)
                    dve.wait_ge(y_t, s.n - 1)
                for t in range(TL):
                    v.tensor_scalar(ys[:, s.par, t, 0:D], rsum[:, t, :], mv[:, t, 0:1], lrs[:, t:t + 1],
                                    ALU.subtract, ALU.mult).then_inc(y_sb, 1)

            def choose(s, k):
                if not has(k, 0, UNITS):
                    return
                dve.wait_ge(lg_ps, s.n + 1)
                settle(dve)
                for t in range(TL):
                    v.max(m8[:, t, :], lbank[:, t * E:(t + 1) * E]).then_inc(rchain, 1)
                dve.wait_ge(rchain, s.n * 11 + TL)
                settle(dve)
                for t in range(TL):
                    v.max_index(i8[:, t, :], m8[:, t, :], lbank[:, t * E:(t + 1) * E]).then_inc(rchain, 1)
                wait(dve, we_sb, s.n)
                v.tensor_tensor(wd[:], m8[:, :, 1], m8[:, :, 0], ALU.subtract).then_inc(wd_sb, 1)
                dve.wait_ge(rchain, s.n * 11 + 8)
                v.tensor_copy(idf[:], i8[:, :, 0:2]).then_inc(rchain, 1)
                dve.wait_ge(rchain, s.n * 11 + 9)
                v.tensor_tensor(oneh[:].rearrange("p t c e -> p (t c) e"),
                                iota_e[:, 0:1, :].to_broadcast([P, TL * 2, E]),
                                idf[:].rearrange("p t c -> p (t c)").unsqueeze(2).to_broadcast([P, TL * 2, E]),
                                ALU.is_equal).then_inc(rchain, 1)
                dve.wait_ge(rchain, s.n * 11 + 10)
                wait(dve, pos_ps, s.n)
                v.tensor_tensor(mask[:], oneh[:, :, 0, :], oneh[:, :, 1, :], ALU.add).then_inc(mask_sb, 1)
                dve.wait_ge(mask_sb, s.n + 1)
                v.tensor_reduce(msum[:], mask[:].rearrange("p t e -> p e t"), AX.X, ALU.add).then_inc(rchain, 1)

            def weights(s, k):
                if not has(k, 0, UNITS):
                    return
                dve.wait_ge(we_sb, s.n + 1)
                v.tensor_scalar(we1[:], we[:], 1.0, None, ALU.add).then_inc(wchain, 1)
                dve.wait_ge(wchain, s.n * 3 + 1)
                v.reciprocal(w0[:], we1[:]).then_inc(wchain, 1)
                dve.wait_ge(wchain, s.n * 3 + 2)
                v.tensor_tensor(w1f[:], w0[:], we[:], ALU.mult).then_inc(wchain, 1)
                dve.wait_ge(wchain, s.n * 3 + 3)
                if k is None or k >= 2:
                    dve.wait_ge(scattered[s.par], s.half * (TL * 2 * 16))
                v.tensor_copy(ys[:, s.par, :, F_EXPERT], idf[:, :, 0]).then_inc(field_sb, 1)
                v.tensor_copy(ys[:, s.par, :, F_W1], w1f[:]).then_inc(field_sb, 1)
                v.tensor_tensor(ys[:, s.par, :, F_DW], w0[:], w1f[:], ALU.subtract).then_inc(field_sb, 1)
                v.tensor_copy(ys[:, s.par, :, F_DEST], dest[:, bass.ds(s.n * TL, TL)]).then_inc(dest_sb, 1)

            def slots(s, k):
                if not has(k, 0, UNITS):
                    return
                dve.wait_ge(pos_ps, s.n + 1)
                v.tensor_tensor(sbase[:], pbank.rearrange("p (t e) -> p t e", e=E),
                                iota_e[:, 1:2, :].to_broadcast([P, TL, E]), ALU.add).then_inc(schain, 1)
                dve.wait_ge(rchain, (s.n + 1) * 11)
                v.tensor_tensor(carry[:], carry[:], msum[:], ALU.add).then_inc(carry_sb, 1)
                dve.wait_ge(schain, s.n * 3 + 1)
                for c in range(2):
                    ins = v.tensor_tensor(sprod[:, :, c, :], oneh[:, :, c, :], sbase[:], ALU.mult)
                ins.then_inc(schain, 1)
                dve.wait_ge(schain, s.n * 3 + 2)
                v.tensor_reduce(slotf[:], sprod[:].rearrange("p t c e -> p (t c) e"), AX.X, ALU.add
                                ).then_inc(schain, 1)
                dve.wait_ge(schain, s.n * 3 + 3)
                v.tensor_copy(slot[:, s.par], slotf[:]).then_inc(slot_sb, 1)

            def body(s, k):
                k1, k2 = (None, None) if k is None else (k - 1, k - 2)
                log_sigmoids(s, k)
                layer_apply(s - 2, k2)
                gates(s, k)
                head_sum(s - 1, k1)
                scan(s, k, (0,))
                scan(s, k, (1,))
                head_apply(s - 1, k1)
                choose(s - 2, k2)
                scan(s, k, (2,))
                apply_gate(s - 1, k1)
                scan(s, k, (3,))
                weights(s - 2, k2)
                slots(s - 2, k2)
                layer_stats(s - 1, k1)
            steps(dve, *SA, body)

            n = [0]

            def link(ins):
                n[0] += 1
                ins.then_inc(tchain, 1)
                dve.wait_ge(tchain, n[0])

            def over_t(a):
                return a.unsqueeze(1).to_broadcast([P, TILES, E])

            def over_e(a):
                return a.unsqueeze(2).to_broadcast([P, TILES, E])

            dve.wait_ge(cnt_ps, 1)
            link(v.tensor_copy(cnt[:], obank[:, 0:E]))
            link(v.tensor_tensor(tbase[:], cnt[:], iota_e[:, 1, :], ALU.add))
            link(v.tensor_scalar(padf[:, 0, :], tbase[:], iop[:], None, ALU.add))
            link(v.tensor_scalar(padf[:, 1, :], padf[:, 0, :], float(P), None, ALU.add))
            v.tensor_copy(padi[:], padf[:]).then_inc(pad_sb, 1)
            link(v.tensor_scalar(cnt[:], cnt[:], float(TS - 1), None, ALU.add))
            link(v.tensor_copy(cnti[:], cnt[:]))
            link(v.tensor_scalar(cnts[:], cnti[:], TS.bit_length() - 1, None, ALU.arith_shift_right))
            link(v.tensor_copy(ntf[:], cnts[:]))
            link(v.tensor_tensor_scan(tend[:], iota_e[:, 2, :], ntf[:], 0.0, ALU.mult, ALU.add))
            link(v.tensor_tensor(tstart[:], tend[:], ntf[:], ALU.subtract))
            link(v.scalar_tensor_tensor(out=tbase[:], in0=tstart[:], scalar=-float(TS), in1=iota_e[:, 1, :],
                                        op0=ALU.mult, op1=ALU.add))
            link(v.tensor_scalar(tbase[:], tbase[:], -float(DUMP), None, ALU.add))
            link(v.tensor_tensor(tge[:], over_e(iot[:]), over_t(tend[:]), ALU.is_ge))
            link(v.tensor_tensor(tgs[:], over_e(iot[:]), over_t(tstart[:]), ALU.is_ge))
            link(v.tensor_tensor(tin[:], tgs[:], tge[:], ALU.subtract))
            link(v.tensor_tensor(tin2[:], tin[:], over_t(tbase[:]), ALU.mult))
            link(v.tensor_reduce(texp[:], tge[:], AX.X, ALU.add))
            link(v.tensor_reduce(tvalid[:], tin[:], AX.X, ALU.add))
            link(v.tensor_reduce(trow[:], tin2[:], AX.X, ALU.add))
            link(v.tensor_scalar(texp[:], texp[:], float(E - 1), None, ALU.min))
            link(v.tensor_tensor(tvalid[:], tvalid[:], iot[:], ALU.mult))
            link(v.scalar_tensor_tensor(out=trow2[:], in0=tvalid[:], scalar=float(TS), in1=trow[:], op0=ALU.mult,
                                        op1=ALU.add))
            link(v.tensor_scalar(trow2[:], trow2[:], float(DUMP), None, ALU.add))
            v.tensor_copy(row_i[:], trow2[:]).then_inc(table_sb, 1)
            v.tensor_copy(exp_i[:], texp[:]).then_inc(table_sb, 1)
            dve.wait_ge(table_sb, 2)
            dve.wait_ge(expert_in, 16 * (1 + E))

            def copy_weights(s, k):
                if not has(k, 0, TILES):
                    return
                e = dve.value_load(exp_i[0:1, bass.ds(s.n, 1)], min_val=0, max_val=E - 1)
                wait(dve, h_ps, (s.n - 1) * 2)
                v.tensor_copy(wb1[:, s.par].rearrange("p f m -> p (f m)"),
                              w1s[:, bass.ds(e, 1), :].rearrange("p a f -> p (a f)")).then_inc(bw_sb, 1)
                wait(dve, by_ps, s.n - 1)
                v.tensor_copy(wb2[:, s.par].rearrange("p f m -> p (f m)"),
                              w2s[:, bass.ds(e, 1), :, :].rearrange("p a f m -> p (a f m)")).then_inc(bw_sb, 1)

            def copy_rows(s, k):
                if has(k, 0, TILES):
                    dve.wait_ge(bx_ps, s.n + 1)
                    wait(dve, h_ps, (s.n - 1) * 2)
                    v.tensor_copy(xbt[:, s.par], ps[:, 4, 0:TS]).then_inc(bx_sb, 1)

            def fields(s, k):
                if not has(k, 0, TILES):
                    return
                dve.wait_ge(rows_in[s.of(RB)], (s.turns(RB) + 1) * 16)
                wait(dve, field_read, s.n)
                v.tensor_scalar(fsel[:], xl[:, s.of(RB), :, F_EXPERT], texp[:, bass.ds(s.n, 1)], None, ALU.is_equal
                                ).then_inc(fchain, 1)
                dve.wait_ge(fchain, s.n * 3 + 1)
                v.tensor_tensor(fwd[:], fsel[:], xl[:, s.of(RB), :, F_DW], ALU.mult).then_inc(fchain, 1)
                dve.wait_ge(fchain, s.n * 3 + 2)
                wait(dve, yo_sb, (s.n - RB + 1) * ST)
                wait(dve, returned[s.of(RB)], s.turns(RB) * (ST * 16))
                v.tensor_tensor(fw[:, s.of(RB)], fwd[:], xl[:, s.of(RB), :, F_W1], ALU.add).then_inc(fchain, 1)
                v.scalar_tensor_tensor(out=fdst[:, s.of(RB)], in0=fsel[:], scalar=-float(TOKENS),
                                       in1=xl[:, s.of(RB), :, F_DEST], op0=ALU.mult, op1=ALU.add
                                       ).then_inc(field_read, 1)

            def copy_out(s, k):
                if has(k, 0, TILES):
                    dve.wait_ge(by_ps, s.n + 1)
                    wait(dve, yo_ps, s.n - 1)
                    v.tensor_copy(ytb[:, s.par], ps[:, 5, 0:TS]).then_inc(by_sb, 1)

            copy_weights(Step(0, 0, RB), 0)
            copy_rows(Step(0, 0, RB), 0)

            def bodyb(s, k):
                k1, kn = (None, None) if k is None else (k - 1, k + 1)
                copy_rows(s + 1, kn)
                copy_weights(s + 1, kn)
                copy_out(s - 1, k1)
                fields(s, k)
            steps(dve, *SB, bodyb)

            def final_stats(s, k):
                if not has(k, 0, GROUPS):
                    return
                dve.wait_ge(ya_sb, s.n + 1)
                yv = ya[:, s.par]
                v.tensor_tensor(yv, yv, yres[:, bass.ds(s.n * CG, CG), :], ALU.add).then_inc(cchain, 1)
                dve.wait_ge(cchain, s.n * (2 * CG + 1) + 1)
                for t in range(CG):
                    v.bn_stats(cs6[:, t, :], yv[:, t, :]).then_inc(cchain, 1)
                dve.wait_ge(cchain, s.n * (2 * CG + 1) + 1 + CG)
                settle(dve)
                for t in range(CG):
                    v.bn_aggr(cmv[:, s.par, t, :], cs6[:, t, :]).then_inc(cchain, 1)

            def final_apply(s, k):
                if not has(k, 0, GROUPS):
                    return
                dve.wait_ge(crs_sb, s.n + 1)
                wait(dve, stored[s.par], s.half * 16)
                for t in range(CG):
                    v.tensor_scalar(co[:, s.par, t, :], ya[:, s.par, t, :], cmv[:, s.par, t, 0:1],
                                    crs[:, t:t + 1], ALU.subtract, ALU.mult).then_inc(co_sb, 1)

            def bodyc(s, k):
                final_stats(s, k)
                final_apply(s - 1, None if k is None else k - 1)
            steps(dve, *SC, bodyc)


_OUT = (TOKENS, D)


def kernel(L0_attn_inputs, L0_attn_Wq, L0_attn_Wk, L0_attn_Wg1, L0_attn_Wg2, L0_attn_Wv, L0_attn_Wg, L0_attn_bg,
           L0_attn_Wo, L0_ffn_gate_w, L0_ffn_w1, L0_ffn_w2):
    import concourse.bacc as _bacc
    from concourse.bass_utils import run_bass_kernel_spmd as _run

    f32 = np.float32
    arrays = {
        "x": np.ascontiguousarray(np.asarray(L0_attn_inputs).reshape(UNITS, TL, P, D).transpose(0, 2, 1, 3)),
        "Wk": np.ascontiguousarray(L0_attn_Wk),
        "Wq": np.ascontiguousarray(L0_attn_Wq),
        "Wg1": np.ascontiguousarray(L0_attn_Wg1),
        "Wg2": np.ascontiguousarray(L0_attn_Wg2),
        "WvG": np.ascontiguousarray(np.asarray(L0_attn_Wv).reshape(D, H, G, 2).transpose(0, 2, 3, 1)),
        "Wg": np.ascontiguousarray(L0_attn_Wg),
        "bg": np.ascontiguousarray(np.asarray(L0_attn_bg).reshape(D, 1)),
        "Wo": np.ascontiguousarray(L0_attn_Wo),
        "gate_wT": np.ascontiguousarray(np.asarray(L0_ffn_gate_w).T),
        "w1": np.ascontiguousarray(L0_ffn_w1),
        "w2": np.ascontiguousarray(L0_ffn_w2),
    }
    head_of_row = np.tile(np.repeat(np.arange(H), DK), 2)
    j_of_row = np.repeat(np.arange(2), HK)
    head_of_col, dv_of_col = np.repeat(np.arange(H), DV), np.tile(np.arange(DV), H)
    same_head = head_of_row[:, None, None] == head_of_col[None, None, :]
    same_dv = (2 * np.arange(G)[None, :, None] + j_of_row[:, None, None]) == dv_of_col[None, None, :]
    arrays["center"] = (same_head * (same_dv - 1.0 / DV)).astype(f32)
    arrays["ident"] = np.eye(P, dtype=f32)
    arrays["tri"] = np.stack([np.triu(np.ones((P, P), f32), 1), np.ones((P, P), f32)], 1)
    arrays["iota8"] = np.broadcast_to(np.stack([np.arange(E), np.arange(E) * REGION, np.ones(E)]).astype(f32),
                                      (P, 3, E)).copy()
    nc = _bacc.Bacc("TRN2", target_bir_lowering=False, num_devices=1)
    aps = {n: nc.dram_tensor(n, a.shape, mybir.dt.from_np(a.dtype), kind="ExternalInput").ap()
           for n, a in arrays.items()}
    out = nc.dram_tensor("out", _OUT, F32, kind="ExternalOutput").ap()
    build(nc, out=out, **aps)
    r = _run(nc, [arrays], core_ids=[0])
    return r.results[0]["out"].reshape(np.asarray(L0_attn_inputs).shape)
```

```python
from contextlib import ExitStack

import concourse.bass as bass
import numpy as np
from concourse import mybir

F32 = mybir.dt.float32
F32R = mybir.dt.float32r
BF16 = mybir.dt.bfloat16
I32 = mybir.dt.int32
U32 = mybir.dt.uint32
ALU = mybir.AluOpType
ACT = mybir.ActivationFunctionType
AX = mybir.AxisListType

P = 128
D = 128
H, DK, DV = 16, 4, 8
HK = H * DK
NB, L = 32, 256
TOKENS = NB * L
E, F = 8, 512
FT = F // P
EPS = 1e-5
GATE_NORM = 16.0

UNIT = 512
TL = UNIT // P
UNITS = TOKENS // UNIT
XB = 4
G = 4

TS = 256
ST = TS // P
TILES = (2 * TOKENS - E) // TS + E
REGION = TOKENS + TS
RB = 4
DUMP = E * REGION
ROW = D + 4
F_DEST, F_EXPERT, F_DW, F_W1 = D, D + 1, D + 2, D + 3
NOWHERE = 1.0e6

CG = 4
TT = TOKENS // P
GROUPS = TT // CG
RC = 8


class Step:

    def __init__(self, i, c, m=2):
        self.i, self.c, self.m = i, c, m

    def __add__(self, k):
        return Step(self.i, self.c + k, self.m)

    def __sub__(self, k):
        return Step(self.i, self.c - k, self.m)

    @property
    def n(self):
        return self.i * self.m + self.c

    def of(self, k):
        return self.c % k

    def turns(self, k):
        return self.i * (self.m // k) + self.c // k

    @property
    def par(self):
        return self.of(2)

    @property
    def half(self):
        return self.turns(2)


def wait(eng, sem, value):
    if isinstance(value, int) and value <= 0:
        return
    eng.wait_ge(sem, value)


def steps(eng, first, loop_from, loop_to, last, m, body):
    loop_to -= (loop_to - loop_from) % m
    for s in range(first, loop_from):
        body(Step(s // m, s % m, m), s)
    with eng.Fori(loop_from // m, loop_to // m) as i:
        for c in range(m):
            body(Step(i, c, m), None)
    for s in range(loop_to, last + 1):
        body(Step(s // m, s % m, m), s)


def has(s, k, count):
    return s is None or 0 <= s - k < count


SETUP = {"ident": P, "Wg1": 16, "Wv": D, "bg": 1}
OTHERS = {"center": G * P, "tri": 2 * P, "numbers": 4 * E, "Wo": D, "gate_w": E}


def build(nc, x, projections, setup, others, Wg2, w1, w2, out):
    with ExitStack() as ctx:
        def sb(name, shape, dt=F32):
            return ctx.enter_context(nc.sbuf_tensor(name, shape, dt))

        def sb_twice(name, rounded, shape):
            with nc.sbuf_tensor(name, shape, F32) as first:
                pass
            return first, sb(rounded, shape, F32R)

        def sem(name):
            return ctx.enter_context(nc.semaphore(name))

        rows = nc.dram_tensor("expert_rows", (DUMP + TS, ROW), F32).ap()
        ybuf = nc.dram_tensor("expert_out", (2 * TOKENS, D), F32).ap()

        ps = ctx.enter_context(nc.psum_tensor("ps", [P, 8, 512], F32))
        kbank, dbank, zbank, qbank = (ps[:, b, :] for b in range(4))
        vbank = (kbank, dbank, qbank, kbank)
        tbank, obank, wbank = ps[:, 4, :], ps[:, 5, :], ps[:, 6, :]
        lbank = ps[:, 7, 0:TL * E]
        pbank = ps[:, 7, 64:64 + TL * E]

        def columns(name, widths):
            whole, parts, at = sb(name, [P, sum(widths.values())]), [], 0
            for width in widths.values():
                parts.append(whole[:, at:at + width])
                at += width
            return whole, parts

        setup_c, (idn, wg1, wv_c, bgc) = columns("setup_c", SETUP)
        others_c, (cen, tri_f, iota_e, wo, gw) = columns("others_c", OTHERS)
        wv = wv_c.rearrange("p (g j h) -> p g j h", g=G, j=2)
        cen = cen.rearrange("p (g d) -> p g d", g=G)
        iota_e = iota_e.rearrange("p (n e) -> p n e", e=E)
        tri_b = sb("tri_b", [P, 2, P], BF16)
        WK, WQ, WG, WD, WV = range(5)
        wx = sb("wx", [P, WV + G, P])
        wxp = sb("wxp", [P, 2, WV + G, P], F32R)
        wg1t = sb("wg1t", [16, P])
        wg2 = sb("wg2", [16, HK])
        nbg = sb("nbg", [P, 1])
        eps = sb("eps", [P, 2])
        w1s, w1lo = sb_twice("w1s", "w1lo", [P, E, F])
        w1hi = sb("w1hi", [P, E, F], F32R)
        w2s = sb("w2s", [P, E, FT, D])

        xs = sb("xs", [P, XB, TL, D])
        xt = sb("xt", [P, 2, 2, UNIT], F32R)
        ks = sb("ks", [P, 2, UNIT])
        qs = sb("qs", [P, 2, UNIT])
        soft = sb("soft", [P, 2, UNIT])
        dec = sb("dec", [P, 2, UNIT])
        kv = sb("kv", [P, G, UNIT])
        state, state_r = sb_twice("state", "state_r", [P, 2, G, UNIT])
        gsig = sb("gsig", [P, UNIT])
        gate = sb("gate", [P, 2, UNIT])
        osq = sb("osq", [P, UNIT])
        hss = sb("hss", [P, TL * H])
        hln = sb("hln", [P, TL * H])
        hrs = sb("hrs", [P, TL * H])
        on = sb("on", [P, 2, UNIT])
        go = sb("go", [P, UNIT])
        st6 = sb("st6", [P, TL, 6])
        mv = sb("mv", [P, TL, 2])
        lln = sb("lln", [P, TL])
        lrs = sb("lrs", [P, TL])
        lsh = sb("lsh", [P, TL])
        ys = sb("ys", [P, 2, TL, ROW])
        yres = sb("yres", [P, TT, D])
        yt = sb("yt", [P, UNIT])
        m8 = sb("m8", [P, TL, 8])
        i8 = sb("i8", [P, TL, 8], U32)
        oneh = sb("oneh", [P, TL, 2, E])
        mask = sb("mask", [P, 2, TL + 1, E], BF16)
        wd = sb("wd", [P, TL])
        we = sb("we", [P, TL])
        we1 = sb("we1", [P, TL])
        w0 = sb("w0", [P, TL])
        sbase = sb("sbase", [P, TL, E])
        sprod = sb("sprod", [P, TL, 2, E])
        slot = sb("slot", [P, 2, TL * 2], I32)
        dest_i = sb("dest_i", [P, TT], I32)
        dest = sb("dest", [P, TT])

        padrow = sb("padrow", [P, ST, ROW])
        iot_i = sb("iot_i", [P, TILES], I32)
        iot = sb("iot", [P, TILES])
        padi = sb("padi", [P, E], I32)
        cnti = sb("cnti", [P, E], I32)
        cnts = sb("cnts", [P, E], I32)
        ntf = sb("ntf", [P, E])
        tend = sb("tend", [P, E])
        tstep = sb("tstep", [P, E])
        flat_kv = kv[:].rearrange("p g t -> p (g t)")
        tge, tgs = (flat_kv[:, k * TILES * E:(k + 1) * TILES * E].rearrange("p (t e) -> p t e", e=E) for k in range(2))
        texp = sb("texp", [P, TILES])
        trow = sb("trow", [P, TILES])
        row_i = sb("row_i", [P, TILES], I32)
        exp_i = sb("exp_i", [P, TILES], I32)

        xl = sb("xl", [P, RB, ST, ROW])
        xb = sb("xb", [P, 2, 2, TS], F32R)
        wb1 = state_r[:, 1].rearrange("p (u a) f -> p u a f", u=2)
        hb = kv[:].rearrange("p (u a) (f t) -> p u (a f) t", u=2, f=2)
        yo = sb("yo", [P, RB, ST, D])
        fsel = sb("fsel", [P, ST])
        fwd = sb("fwd", [P, ST])
        fw = sb("fw", [P, RB, ST])
        fdst = sb("fdst", [P, RB, ST], I32)

        y0 = state[:].rearrange("p u g (t d) -> p (u g) t d", d=D)
        y1 = w1s[:].rearrange("p r (t d) -> p r t d", d=D)
        cs6 = sb("cs6", [P, CG, 6])
        cmv = sb("cmv", [P, 2, CG, 2])
        cln = sb("cln", [P, CG])
        crs = sb("crs", [P, 2, CG])
        csh = sb("csh", [P, 2, CG])

        const_in = sem("const_in")
        expert_in = sem("expert_in")
        dump_in = sem("dump_in")
        x_in = [sem(f"x_in{k}") for k in range(XB)]
        setup_pool = sem("setup_pool")
        setup_dve, late_dve = sem("setup_dve"), sem("late_dve")
        nbg_sb = sem("nbg_sb")
        pool_passed, dve_passed = sem("pool_passed"), sem("dve_passed")
        wg1t_ps = sem("wg1t_ps")
        wdec_ps = sem("wdec_ps")
        xt_ps, xt_sb, xrest_sb = sem("xt_ps"), sem("xt_sb"), sem("xrest_sb")
        k_ps, d_ps, q_ps, z_ps, v_ps = (sem(s) for s in ("k_ps", "d_ps", "q_ps", "z_ps", "v_ps"))
        k_sb, q_sb = sem("k_sb"), sem("q_sb")
        abs_sb, sexp_sb, sln_sb, lsd_sb, lsz_sb, dec_sb, gsig_sb, gate_sb = (
            sem(s) for s in ("abs_sb", "sexp_sb", "sln_sb", "lsd_sb", "lsz_sb", "dec_sb", "gsig_sb", "gate_sb"))
        kv_sb, scan_sb, qst_sb = sem("kv_sb"), sem("scan_sb"), sem("qst_sb")
        o_ps, osq_sb, hss_sb, hln_sb, hrs_sb, on_sb = (
            sem(s) for s in ("o_ps", "osq_sb", "hss_sb", "hln_sb", "hrs_sb", "on_sb"))
        on_t, go_sb, wo_ps = sem("on_t"), sem("go_sb"), sem("wo_ps")
        lchain, lln_sb, lrs_sb, lsh_sb, y_sb = (
            sem(s) for s in ("lchain", "lln_sb", "lrs_sb", "lsh_sb", "y_sb"))
        w1hi_sb, w1lo_sb = sem("w1hi_sb"), sem("w1lo_sb")
        y_t, yt_sb, lg_ps, yres_sb = sem("y_t"), sem("yt_sb"), sem("lg_ps"), sem("yres_sb")
        rchain, mask_sb, wd_sb, we_sb, wchain = (
            sem(s) for s in ("rchain", "mask_sb", "wd_sb", "we_sb", "wchain"))
        carry_sb, pos_ps, schain, slot_sb, field_sb, ef_sb, dest_sb = (
            sem(s) for s in ("carry_sb", "pos_ps", "schain", "slot_sb", "field_sb", "ef_sb", "dest_sb"))
        scattered = [sem("scattered0"), sem("scattered1")]
        cnt_ps, tchain, pad_sb, table_sb, padded = (
            sem(s) for s in ("cnt_ps", "tchain", "pad_sb", "table_sb", "padded"))
        rows_in = [sem(f"rows_in{k}") for k in range(RB)]
        bx_ps, bx_sb, bw_sb = sem("bx_ps"), sem("bx_sb"), sem("bw_sb")
        h_ps, h_sb, yo_ps, yo_sb = (sem(s) for s in ("h_ps", "h_sb", "yo_ps", "yo_sb"))
        fchain, field_read = sem("fchain"), sem("field_read")
        returned = [sem(f"returned{k}") for k in range(RB)]
        y_in = [sem(f"y_in{k}") for k in range(RC)]
        ya_sb, yr_sb, cchain, cln_sb, crs_sb, csh_sb, co_sb, cl_sb = (
            sem(s) for s in ("ya_sb", "yr_sb", "cchain", "cln_sb", "crs_sb", "csh_sb", "co_sb", "cl_sb"))
        stored = sem("stored")

        CONSTS = [(setup_c[:], setup), (wg2[:], Wg2), (wx[:, WK:WG + 1, :], projections), (others_c[:], others)]
        SET_UP = 8 + G
        SA = (0, 4, UNITS - 2, UNITS + 1, 2)
        SB = (0, 4, TILES - 1, TILES + 1, RB)
        SC = (0, RC, GROUPS, GROUPS - 1, RC)

        block = ctx.enter_context(nc.Block())

        def settle(eng):
            eng.sem_inc(pool_passed if eng is nc.gpsimd else dve_passed, 1)

        @block.sync
        def _(sp):
            def load_x(s, k):
                if not has(k, 0, UNITS):
                    return
                wait(sp, wo_ps, s.n - XB + 1)
                sp.dma_start(xs[:, s.of(XB)], x[bass.ds(s.n, 1)].rearrange("u p t d -> (u p) t d")
                             ).then_inc(x_in[s.of(XB)], 16)

            load_x(Step(0, 0, XB), 0)
            for dst, src in CONSTS:
                sp.dma_start(dst, src).then_inc(const_in, 16)
            for k in range(1, XB):
                load_x(Step(0, k, XB), k)
            sp.dma_start(w1s[:], w1.rearrange("e d f -> d e f")).then_inc(expert_in, 16)
            for e in range(E):
                sp.dma_start(w2s[:, e], w2[e].rearrange("(t p) d -> p t d", p=P)).then_inc(expert_in, 16)
            sp.wait_ge(setup_pool, 4)
            sp.dma_start(rows[DUMP:DUMP + TS, :].rearrange("(p t) d -> p t d", p=P), padrow[:]).then_inc(dump_in, 16)

            steps(sp, XB, XB, UNITS, UNITS - 1, XB, load_x)

            sp.wait_ge(pad_sb, 1)
            for e in range(E):
                at = sp.value_load(padi[0:1, e:e + 1], min_val=0, max_val=DUMP - TS)
                sp.dma_start(rows[bass.ds(at, TS), :].rearrange("(p t) d -> p t d", p=P),
                             padrow[:]).then_inc(padded, 16)

            for q in scattered:
                sp.wait_ge(q, UNITS // 2 * TL * 2 * 16)
            sp.wait_ge(padded, 16 * E)
            sp.wait_ge(dump_in, 16)
            sp.wait_ge(table_sb, 2)

            def load_rows(s, k):
                if not has(k, 0, TILES):
                    return
                wait(sp, bx_ps, s.n - RB + 1)
                wait(sp, field_read, s.n - RB + 1)
                at = sp.value_load(row_i[0:1, bass.ds(s.n, 1)], min_val=0, max_val=DUMP)
                sp.dma_start(xl[:, s.of(RB)], rows[bass.ds(at, TS), :].rearrange("(p t) d -> p t d", p=P)
                             ).then_inc(rows_in[s.of(RB)], 16)
            steps(sp, 0, 4, TILES, TILES - 1, RB, load_rows)

            for r, q in enumerate(returned):
                sp.wait_ge(q, len(range(r, TILES, RB)) * ST * 16)
            yv = ybuf.rearrange("(c p t) d -> c p (t d)", c=2, p=P)

            def load_y(s, k):
                if has(k, 0, GROUPS):
                    wait(sp, yr_sb, s.n - RC + 1)
                    for c, buf in enumerate((y0, y1)):
                        sp.dma_start(buf[:, s.of(RC)].rearrange("p t d -> p (t d)"),
                                     yv[c, :, bass.ds(s.n * (CG * D), CG * D)]).then_inc(y_in[s.of(RC)], 16)

            steps(sp, 0, RC, GROUPS, GROUPS - 1, RC, load_y)

        @block.gpsimd
        def _(pool):
            nc.gpsimd.memset(padrow[:, :, 0:D], 0.0).then_inc(setup_pool, 1)
            nc.gpsimd.memset(padrow[:, :, F_DW:ROW], 0.0).then_inc(setup_pool, 1)
            nc.gpsimd.memset(padrow[:, :, F_DEST:F_DEST + 1], NOWHERE).then_inc(setup_pool, 1)
            nc.gpsimd.memset(padrow[:, :, F_EXPERT:F_EXPERT + 1], -1.0).then_inc(setup_pool, 1)
            nc.gpsimd.iota(iot_i[:], [[1, TILES]], base=0, channel_multiplier=0).then_inc(setup_pool, 1)
            nc.gpsimd.iota(dest_i[:], [[1, TT]], base=TOKENS, channel_multiplier=TT).then_inc(setup_pool, 1)

            def products(s, k):
                if not has(k, 0, UNITS):
                    return
                pool.wait_ge(q_sb, s.n + 1)
                for g in range(G):
                    pool.wait_ge(scan_sb, s.n * G + g + 1)
                    nc.gpsimd.tensor_tensor(state[:, s.par, g], qs[:, s.par], state[:, s.par, g],
                                            ALU.mult).then_inc(qst_sb, 1)

            def scatter(s, k):
                if not has(k, 0, UNITS):
                    return
                pool.wait_ge(y_sb, (s.n + 1) * TL)
                pool.wait_ge(field_sb, (s.n + 1) * 2)
                pool.wait_ge(ef_sb, s.n + 1)
                pool.wait_ge(dest_sb, s.n + 1)
                pool.wait_ge(slot_sb, s.n + 1)
                settle(pool)
                for t in range(TL):
                    for c in range(2):
                        m = 2 * t + c
                        pool.indirect_dma_start(
                            out=rows, out_offset=bass.IndirectOffsetOnAxis(ap=slot[:, s.par, m:m + 1], axis=0),
                            in_=ys[:, s.par, t, :], in_offset=None).then_inc(scattered[s.par], 16)

            def body(s, k):
                products(s, k)
                scatter(s - 2, None if k is None else k - 2)
            steps(pool, *SA, body)

            def give_back(s, k):
                if not has(k, 2, TILES):
                    return
                s = s - 2
                pool.wait_ge(yo_sb, (s.n + 1) * ST)
                settle(pool)
                for t in range(ST):
                    pool.indirect_dma_start(
                        out=ybuf, out_offset=bass.IndirectOffsetOnAxis(ap=fdst[:, s.of(RB), t:t + 1], axis=0),
                        in_=yo[:, s.of(RB), t, :], in_offset=None, bounds_check=2 * TOKENS - 1,
                        oob_is_err=False).then_inc(returned[s.of(RB)], 16)
            steps(pool, *SB, give_back)

            def add_up(s, k):
                if not has(k, 0, GROUPS):
                    return
                pool.wait_ge(y_in[s.of(RC)], (s.turns(RC) + 1) * 32)
                nc.gpsimd.tensor_tensor(y0[:, s.of(RC)], y0[:, s.of(RC)], y1[:, s.of(RC)], ALU.add
                                        ).then_inc(ya_sb, 1)
            steps(pool, *SC, add_up)

        @block.scalar
        def _(act):
            nc.scalar.preload_act_table_set("natural_log_exp_and_others")
            act.wait_ge(const_in, 16 * len(CONSTS))
            nc.scalar.activation(nbg[:], bgc, ACT.Copy, scale=-1.0).then_inc(nbg_sb, 1)
            def copy_xt(s, k):
                if has(k, 0, UNITS):
                    act.wait_ge(xt_ps, s.n + 1)
                    wait(act, v_ps, (s.n - 1) * G)
                    nc.scalar.activation(xt[:, s.par, 0], tbank, ACT.Copy).then_inc(xt_sb, 1)

            def softplus_in(s, k):
                if not has(k, 0, UNITS):
                    return
                act.wait_ge(d_ps, s.n + 1)
                wait(act, dec_sb, s.n)
                nc.scalar.activation(soft[:, 0], dbank, ACT.Abs).then_inc(abs_sb, 1)
                act.wait_ge(z_ps, s.n + 1)
                wait(act, gsig_sb, s.n)
                nc.scalar.activation(soft[:, 1], zbank, ACT.Abs, bias=bgc).then_inc(abs_sb, 1)

            def softplus(s, k):
                if not has(k, 0, UNITS):
                    return
                act.wait_ge(abs_sb, s.n * 2 + 2)
                nc.scalar.activation(soft[:], soft[:], ACT.Exp, scale=-1.0).then_inc(sexp_sb, 1)
                act.wait_ge(sexp_sb, s.n + 1)
                nc.scalar.activation(soft[:], soft[:], ACT.Ln, bias=1.0).then_inc(sln_sb, 1)

            def copy_k(s, k):
                if has(k, 0, UNITS):
                    act.wait_ge(k_ps, s.n + 1)
                    wait(act, kv_sb, (s.n - 1) * G)
                    nc.scalar.activation(ks[:, s.par], kbank, ACT.Copy, scale=DK ** -0.5).then_inc(k_sb, 1)

            def decay_exp(s, k):
                if not has(k, 0, UNITS):
                    return
                act.wait_ge(lsd_sb, s.n + 1)
                wait(act, scan_sb, (s.n - 1) * G)
                nc.scalar.activation(dec[:, s.par].rearrange("p (b l) -> p b l", l=L)[:, :, 1:],
                                     soft[:, 0].rearrange("p (b l) -> p b l", l=L)[:, :, 1:],
                                     ACT.Exp, scale=1.0 / GATE_NORM).then_inc(dec_sb, 1)

            def gate_exp(s, k):
                if has(k, 0, UNITS):
                    act.wait_ge(lsz_sb, s.n + 1)
                    wait(act, gate_sb, s.n)
                    nc.scalar.activation(gsig[:], soft[:, 1], ACT.Exp, bias=bgc).then_inc(gsig_sb, 1)

            def copy_q(s, k):
                if has(k, 0, UNITS):
                    act.wait_ge(q_ps, s.n + 1)
                    wait(act, qst_sb, (s.n - 1) * G)
                    nc.scalar.activation(qs[:, s.par], qbank, ACT.Copy).then_inc(q_sb, 1)

            def square(s, k):
                if has(k, 0, UNITS):
                    act.wait_ge(o_ps, s.n + 1)
                    wait(act, on_sb, s.n)
                    nc.scalar.activation(osq[:], obank, ACT.Square).then_inc(osq_sb, 1)

            def root(src, tmp, dst, bias, tmp_sb, dst_sb, n):
                nc.scalar.activation(tmp, src, ACT.Ln, bias=bias).then_inc(tmp_sb, 1)
                act.wait_ge(tmp_sb, n + 1)
                nc.scalar.activation(dst, tmp, ACT.Exp, scale=-0.5).then_inc(dst_sb, 1)

            def head_root(s, k):
                if has(k, 0, UNITS):
                    act.wait_ge(hss_sb, s.n + 1)
                    wait(act, on_sb, s.n)
                    root(hss[:], hln[:], hrs[:], eps[:, 1:2], hln_sb, hrs_sb, s.n)

            def layer_root(s, k):
                if has(k, 0, UNITS):
                    act.wait_ge(lchain, (s.n + 1) * 8)
                    wait(act, y_sb, s.n * TL)
                    root(mv[:, :, 1], lln[:], lrs[:], eps[:, 0:1], lln_sb, lrs_sb, s.n)

            def layer_apply(s, k):
                if not has(k, 0, UNITS):
                    return
                act.wait_ge(lsh_sb, s.n + 1)
                if k is None or k >= 2:
                    act.wait_ge(scattered[s.par], s.half * (TL * 2 * 16))
                    act.wait_ge(yres_sb, s.n - 1)
                    act.wait_ge(y_t, s.n - 1)
                for t in range(TL):
                    nc.scalar.activation(ys[:, s.par, t, 0:D], wbank[:, t * D:(t + 1) * D], ACT.Identity,
                                         bias=lsh[:, t:t + 1], scale=lrs[:, t:t + 1]).then_inc(y_sb, 1)

            def split_lead():
                act.wait_ge(expert_in, 16 * (1 + E))
                for e in range(0, E, 2):
                    nc.scalar.activation(w1hi[:, e:e + 2, :], w1s[:, e:e + 2, :], ACT.Copy).then_inc(w1hi_sb, 1)

            def copy_yt(s, k):
                if has(k, 0, UNITS):
                    act.wait_ge(y_t, s.n + 1)
                    wait(act, lg_ps, s.n)
                    nc.scalar.activation(yt[:], tbank, ACT.Copy).then_inc(yt_sb, 1)

            def keep_y(s, k):
                if has(k, 0, UNITS):
                    act.wait_ge(y_sb, (s.n + 1) * TL)
                    nc.scalar.activation(yres[:, bass.ds(s.n * TL, TL), :], ys[:, s.par, :, 0:D],
                                         ACT.Copy).then_inc(yres_sb, 1)

            def weight_exp(s, k):
                if has(k, 0, UNITS):
                    act.wait_ge(wd_sb, s.n + 1)
                    wait(act, field_sb, s.n * 2)
                    nc.scalar.activation(we[:], wd[:], ACT.Exp).then_inc(we_sb, 1)

            def row_fields(s, k):
                if not has(k, 0, UNITS):
                    return
                act.wait_ge(rchain, s.n * 9 + 8)
                if k is None or k >= 2:
                    act.wait_ge(scattered[s.par], s.half * (TL * 2 * 16))
                nc.scalar.activation(ys[:, s.par, :, F_DEST], dest[:, bass.ds(s.n * TL, TL)], ACT.Copy
                                     ).then_inc(dest_sb, 1)
                nc.scalar.activation(ys[:, s.par, :, F_EXPERT], i8[:, :, 0], ACT.Copy).then_inc(ef_sb, 1)

            copy_xt(Step(0, 0), 0)
            act.wait_ge(setup_dve, SET_UP)
            for stage in (copy_k, softplus_in, copy_q, softplus):
                stage(Step(0, 0), 0)

            def body(s, k):
                k1, k2, kn = (None,) * 3 if k is None else (k - 1, k - 2, k + 1)
                decay_exp(s, k)
                layer_apply(s - 2, k2)
                square(s - 1, k1)
                copy_yt(s - 2, k2)
                gate_exp(s, k)
                head_root(s - 1, k1)
                copy_xt(s + 1, kn)
                keep_y(s - 2, k2)
                copy_k(s + 1, kn)
                softplus_in(s + 1, kn)
                weight_exp(s - 2, k2)
                copy_q(s + 1, kn)
                row_fields(s - 2, k2)
                if k == UNITS:
                    split_lead()
                softplus(s + 1, kn)
                layer_root(s - 1, k1)
            steps(act, *SA, body)

            nc.scalar.preload_act_table(ACT.Silu)

            def silu(s, k):
                if not has(k, 0, TILES):
                    return
                for b in range(2):
                    act.wait_ge(h_ps, s.n * 2 + b + 1)
                    if b == 0:
                        wait(act, yo_ps, s.n - 1)
                    nc.scalar.activation(hb[:, s.par, 2 * b:2 * b + 2, :].rearrange("p f t -> p (f t)"),
                                         ps[:, 2 * s.par + b, :], ACT.Silu).then_inc(h_sb, 1)

            def weigh(s, k):
                if not has(k, 0, TILES):
                    return
                act.wait_ge(yo_ps, s.n + 1)
                act.wait_ge(fchain, (s.n + 1) * 3)
                act.wait_ge(field_read, s.n + 1)
                wait(act, returned[s.of(RB)], s.turns(RB) * (ST * 16))
                for t in range(ST):
                    nc.scalar.activation(yo[:, s.of(RB), t, :], ps[:, 5 + s.par, t * D:(t + 1) * D], ACT.Copy,
                                         scale=fw[:, s.of(RB), t:t + 1]).then_inc(yo_sb, 1)

            def bodyb(s, k):
                weigh(s - 2, None if k is None else k - 2)
                silu(s, k)
            steps(act, *SB, bodyb)

            nc.scalar.preload_act_table_set("natural_log_exp_and_others")

            def final_root(s, k):
                if has(k, 0, GROUPS):
                    act.wait_ge(cchain, (s.n + 1) * (2 * CG))
                    wait(act, co_sb, (s.n - 1) * (CG - 1))
                    wait(act, crs_sb, s.n)
                    root(cmv[:, s.par, :, 1], cln[:], crs[:, s.par], eps[:, 0:1], cln_sb, crs_sb, s.n)

            def final_apply(s, k):
                if has(k, 0, GROUPS):
                    act.wait_ge(csh_sb, s.n + 1)
                    for t in range(CG - 1):
                        row = yres[:, bass.ds(s.n * CG + t, 1), :].rearrange("p a d -> p (a d)")
                        nc.scalar.activation(row, row, ACT.Identity, bias=csh[:, s.par, t:t + 1],
                                             scale=crs[:, s.par, t:t + 1]).then_inc(co_sb, 1)

            def store(s, k):
                if has(k, 0, GROUPS):
                    act.wait_ge(co_sb, (s.n + 1) * (CG - 1))
                    act.wait_ge(cl_sb, s.n + 1)
                    act.dma_start(out[:, bass.ds(s.n * CG, CG), :], yres[:, bass.ds(s.n * CG, CG), :]
                                  ).then_inc(stored, 16)

            def bodyc(s, k):
                k1, k2 = (None, None) if k is None else (k - 1, k - 2)
                final_root(s, k)
                final_apply(s - 1, k1)
                store(s - 2, k2)
            steps(act, 0, 4, GROUPS, GROUPS + 1, 4, bodyc)
            act.wait_ge(stored, GROUPS * 16)

        @block.tensor
        def _(pe):
            pe.wait_ge(const_in, 16 * len(CONSTS))

            def turn(bank, src, tiles, done):
                for t in range(tiles):
                    mm = nc.tensor.transpose(bank[:, t * P:(t + 1) * P], src(t), idn)
                mm.then_inc(done, 1)

            def turn_x(s, k):
                if has(k, 0, UNITS):
                    pe.wait_ge(x_in[s.of(XB)], (s.turns(XB) + 1) * 16)
                    wait(pe, yt_sb, s.n - 2)
                    turn(tbank, lambda t: xs[:, s.of(XB), t, :], TL, xt_ps)

            PARTS = ((0, 0), (1, 0), (0, 1))

            def project(s, bank, w, done):
                for m, (a, b) in enumerate(PARTS):
                    if done is k_ps and m == 2:
                        pe.wait_ge(xrest_sb, s.n + 1)
                    mm = nc.tensor.matmul(bank, wxp[:, a, w, :], xt[:, s.par, b], start=(m == 0), stop=(m == 2))
                mm.then_inc(done, 1)

            def keys(s, k):
                if has(k, 0, UNITS):
                    pe.wait_ge(xt_sb, s.n + 1)
                    wait(pe, kv_sb, s.n * G)
                    project(s, kbank, WK, k_ps)

            def decays(s, k):
                if has(k, 0, UNITS):
                    wait(pe, kv_sb, (s.n - 1) * G + 2)
                    project(s, dbank, WD, d_ps)

            def queries(s, k):
                if has(k, 0, UNITS):
                    wait(pe, kv_sb, (s.n - 1) * G + 3)
                    project(s, qbank, WQ, q_ps)

            def gate_inputs(s, k):
                if has(k, 0, UNITS):
                    wait(pe, gate_sb, s.n)
                    project(s, zbank, WG, z_ps)

            def values(s, k, g):
                if has(k, 0, UNITS):
                    free = (k_sb, lsd_sb, q_sb, kv_sb)[g]
                    pe.wait_ge(free, s.n * G + 1 if g == 3 else s.n + 1)
                    project(s, vbank[g], WV + g, v_ps)

            def heads(s, k):
                if not has(k, 0, UNITS):
                    return
                pe.wait_ge(qst_sb, (s.n + 1) * G)
                wait(pe, on_sb, s.n)
                for t in range(TL):
                    for g in range(G):
                        mm = nc.tensor.matmul(obank[:, t * P:(t + 1) * P], state[:, s.par, g, t * P:(t + 1) * P],
                                              cen[:, g, :], start=(g == 0), stop=(g == G - 1))
                mm.then_inc(o_ps, 1)

            def turn_o(s, k):
                if has(k, 0, UNITS):
                    pe.wait_ge(on_sb, s.n + 1)
                    wait(pe, yt_sb, s.n)
                    wait(pe, xrest_sb, s.n + 3 if k is None else min(s.n + 3, UNITS))
                    turn(tbank, lambda t: on[:, s.par, t * P:(t + 1) * P], TL, on_t)

            def residual(s, k):
                if has(k, 0, UNITS):
                    wait(pe, y_sb, s.n * TL)
                    nc.tensor.matmul(wbank, idn, xs[:, s.of(XB)].rearrange("p t d -> p (t d)"),
                                     start=True, stop=False)

            def project_o(s, k):
                if not has(k, 0, UNITS):
                    return
                pe.wait_ge(go_sb, s.n + 1)
                for t in range(TL):
                    mm = nc.tensor.matmul(wbank[:, t * P:(t + 1) * P], go[:, t * P:(t + 1) * P], wo,
                                          start=False, stop=(t == TL - 1))
                mm.then_inc(wo_ps, 1)

            def turn_y(s, k):
                if has(k, 0, UNITS):
                    pe.wait_ge(y_sb, (s.n + 1) * TL)
                    pe.wait_ge(go_sb, s.n + 1)
                    turn(tbank, lambda t: ys[:, s.par, t, 0:D], TL, y_t)

            def logits(s, k):
                if not has(k, 0, UNITS):
                    return
                pe.wait_ge(yt_sb, s.n + 1)
                wait(pe, schain, s.n * 2)
                for t in range(TL):
                    mm = nc.tensor.matmul(lbank[:, t * E:(t + 1) * E], yt[:, t * P:(t + 1) * P], gw,
                                          start=True, stop=True)
                mm.then_inc(lg_ps, 1)

            def positions(s, k):
                if not has(k, 0, UNITS):
                    return
                pe.wait_ge(mask_sb, s.n + 1)
                wait(pe, carry_sb, s.n + 1)
                m = mask[:, s.par].rearrange("p t e -> p (t e)")
                nc.tensor.matmul(pbank, tri_b[:, 0, :], m[:, 0:TL * E], start=True, stop=False)
                for t in range(1, TL):
                    nc.tensor.matmul(pbank[:, t * E:], tri_b[:, 1, :], m[:, 0:(TL - t) * E],
                                     start=False, stop=False)
                for t in range(TL):
                    mm = nc.tensor.matmul(pbank[:, t * E:(t + 1) * E], tri_b[:, 1, :], m[:, TL * E:],
                                          start=False, stop=(t == TL - 1))
                mm.then_inc(pos_ps, 1)

            nc.tensor.transpose(tbank[0:16, 0:P], wg1, idn).then_inc(wg1t_ps, 1)
            pe.wait_ge(setup_dve, 1)
            nc.tensor.matmul(obank[:, 0:HK], wg1t[:], wg2[:], start=True, stop=True).then_inc(wdec_ps, 1)
            turn_x(Step(0, 0, XB), 0)
            pe.wait_ge(setup_dve, SET_UP)
            for stage in (keys, decays, gate_inputs, queries):
                stage(Step(0, 0, XB), 0)
            pe.wait_ge(setup_dve, SET_UP + 1)
            values(Step(0, 0, XB), 0, 0)

            def body(s, k):
                k1, k2, kn = (None,) * 3 if k is None else (k - 1, k - 2, k + 1)
                values(s, k, 1)
                turn_y(s - 2, k2)
                values(s, k, 2)
                values(s, k, 3)
                turn_x(s + 1, kn)
                logits(s - 2, k2)
                residual(s - 1, k1)
                keys(s + 1, kn)
                turn_o(s - 1, k1)
                decays(s + 1, kn)
                gate_inputs(s + 1, kn)
                queries(s + 1, kn)
                positions(s - 2, k2)
                project_o(s - 1, k1)
                values(s + 1, kn, 0)
                heads(s, k)
            steps(pe, 0, XB, UNITS - 2, UNITS + 1, XB, body)

            pe.wait_ge(carry_sb, UNITS + 1)
            nc.tensor.matmul(obank[:, 0:E], tri_b[:, 1, :], mask[:, UNITS % 2, TL, :], start=True, stop=True
                             ).then_inc(cnt_ps, 1)

            def turn_rows(s, k):
                if has(k, 0, TILES):
                    pe.wait_ge(rows_in[s.of(RB)], (s.turns(RB) + 1) * 16)
                    wait(pe, bx_sb, (s.n - 1) * 2)
                    turn(ps[:, 4 + 3 * s.par, :], lambda t: xl[:, s.of(RB), t, 0:D], ST, bx_ps)

            def hidden(s, k):
                if not has(k, 0, TILES):
                    return
                pe.wait_ge(bx_sb, (s.n + 1) * 2)
                pe.wait_ge(bw_sb, s.n + 1)
                wait(pe, h_sb, (s.n - 1) * 2)
                for f in range(FT):
                    for m, (a, b) in enumerate(PARTS):
                        mm = nc.tensor.matmul(ps[:, 2 * s.par + f // 2, (f % 2) * TS:(f % 2 + 1) * TS],
                                              wb1[:, s.par, a, f * P:(f + 1) * P], xb[:, s.par, b, :],
                                              start=(m == 0), stop=(m == 2))
                    if f % 2:
                        mm.then_inc(h_ps, 1)

            def outputs(s, k):
                if not has(k, 0, TILES):
                    return
                e = pe.value_load(exp_i[0:1, bass.ds(s.n, 1)], min_val=0, max_val=E - 1)
                pe.wait_ge(h_sb, (s.n + 1) * 2)
                wait(pe, yo_sb, (s.n - 1) * ST)
                for t in range(ST):
                    for f in range(FT):
                        mm = nc.tensor.matmul(
                            ps[:, 5 + s.par, t * P:(t + 1) * P], hb[:, s.par, f, t * P:(t + 1) * P],
                            w2s[:, bass.ds(e, 1), f, :].rearrange("p a d -> p (a d)"),
                            start=(f == 0), stop=(f == FT - 1))
                mm.then_inc(yo_ps, 1)

            pe.wait_ge(table_sb, 2)
            turn_rows(Step(0, 0, RB), 0)

            def bodyb(s, k):
                k1, k2, kn = (None,) * 3 if k is None else (k - 1, k - 2, k + 1)
                turn_rows(s + 1, kn)
                hidden(s, k)
                outputs(s - 1, k1)
            steps(pe, *SB, bodyb)

        @block.vector
        def _(dve):
            v = nc.vector
            dve.wait_ge(const_in, 16 * len(CONSTS))
            dve.wait_ge(nbg_sb, 1)
            dve.wait_ge(wg1t_ps, 1)
            v.tensor_copy(wg1t[:], tbank[0:16, 0:P]).then_inc(setup_dve, 1)
            for g in range(G):
                v.tensor_copy(wx[:, WV + g, :].rearrange("p (a k) -> p a k", k=DK),
                              wv[:, g].rearrange("p j h -> p (j h)").unsqueeze(2).to_broadcast([P, 2 * H, DK])
                              ).then_inc(setup_dve, 1)
            dve.wait_ge(wdec_ps, 1)
            for j in range(2):
                v.tensor_copy(wx[:, WD, j * HK:(j + 1) * HK], obank[:, 0:HK]).then_inc(setup_dve, 1)
            dve.wait_ge(setup_dve, 3 + G)
            v.tensor_copy(wxp[:, 0], wx[:]).then_inc(setup_dve, 1)
            v.memset(dec[:].rearrange("p u (b l) -> p u b l", l=L)[:, :, :, 0:1], 0.0).then_inc(setup_dve, 1)
            v.memset(eps[:, 0:1], EPS).then_inc(setup_dve, 1)
            v.memset(eps[:, 1:2], DV * EPS).then_inc(setup_dve, 1)
            dve.wait_ge(setup_dve, 7 + G)
            v.tensor_tensor(wxp[:, 1, 0:WV], wx[:, 0:WV], wxp[:, 0, 0:WV].bitcast(F32), ALU.subtract
                            ).then_inc(setup_dve, 1)

            def log_sigmoid_d(s, k):
                if has(k, 0, UNITS):
                    dve.wait_ge(sln_sb, s.n + 1)
                    v.scalar_tensor_tensor(out=soft[:, 0], in0=dbank, scalar=0.0, in1=soft[:, 0], op0=ALU.min,
                                           op1=ALU.subtract).then_inc(lsd_sb, 1)

            def log_sigmoid_z(s, k):
                if has(k, 0, UNITS):
                    v.scalar_tensor_tensor(out=soft[:, 1], in0=zbank, scalar=nbg[:], in1=soft[:, 1], op0=ALU.min,
                                           op1=ALU.subtract).then_inc(lsz_sb, 1)

            def split_x(s, k):
                if has(k, 0, UNITS):
                    dve.wait_ge(xt_sb, s.n + 1)
                    v.tensor_tensor(xt[:, s.par, 1], tbank, xt[:, s.par, 0].bitcast(F32), ALU.subtract
                                    ).then_inc(xrest_sb, 1)

            def split_rest():
                for n, e in enumerate(range(0, E, 2)):
                    dve.wait_ge(w1hi_sb, n + 1)
                    v.tensor_tensor(w1lo[:, e:e + 2, :], w1s[:, e:e + 2, :], w1hi[:, e:e + 2, :].bitcast(F32),
                                    ALU.subtract).then_inc(w1lo_sb, 1)

            def keys_values(s, k, g):
                if has(k, 0, UNITS):
                    if g == 0:
                        dve.wait_ge(k_sb, s.n + 1)
                    dve.wait_ge(v_ps, s.n * G + g + 1)
                    wait(dve, scan_sb, (s.n - 1) * G + g + 1)
                    v.tensor_tensor(kv[:, g], vbank[g], ks[:, s.par], ALU.mult).then_inc(kv_sb, 1)

            def scan(s, k, g):
                if has(k, 0, UNITS):
                    dve.wait_ge(kv_sb, s.n * G + g + 1)
                    dve.wait_ge(dec_sb, s.n + 1)
                    wait(dve, o_ps, s.n - 1)
                    v.tensor_tensor_scan(state[:, s.par, g], dec[:, s.par], kv[:, g], 0.0,
                                         ALU.mult, ALU.add).then_inc(scan_sb, 1)

            def gates(s, k):
                if not has(k, 0, UNITS):
                    return
                dve.wait_ge(gsig_sb, s.n + 1)
                v.scalar_tensor_tensor(out=gate[:, s.par], in0=zbank, scalar=bgc, in1=gsig[:], op0=ALU.add,
                                       op1=ALU.mult).then_inc(gate_sb, 1)

            def head_sum(s, k):
                if has(k, 0, UNITS):
                    dve.wait_ge(osq_sb, s.n + 1)
                    wait(dve, hln_sb, s.n)
                    v.tensor_reduce(hss[:], osq[:].rearrange("p (h e) -> p h e", e=DV), AX.X, ALU.add
                                    ).then_inc(hss_sb, 1)

            def head_apply(s, k):
                if has(k, 0, UNITS):
                    dve.wait_ge(hrs_sb, s.n + 1)
                    wait(dve, on_t, s.n - 1)
                    v.scalar_tensor_tensor(out=on[:, s.par].rearrange("p (h e) -> p h e", e=DV),
                                           in0=obank.rearrange("p (h e) -> p h e", e=DV), scalar=DV ** 0.5,
                                           in1=hrs[:].unsqueeze(2).to_broadcast([P, TL * H, DV]),
                                           op0=ALU.mult, op1=ALU.mult).then_inc(on_sb, 1)

            def apply_gate(s, k):
                if has(k, 0, UNITS):
                    dve.wait_ge(on_t, s.n + 1)
                    dve.wait_ge(gate_sb, s.n + 1)
                    wait(dve, wo_ps, s.n)
                    v.tensor_tensor(go[:], tbank, gate[:, s.par], ALU.mult).then_inc(go_sb, 1)

            def layer_stats(s, k):
                if not has(k, 0, UNITS):
                    return
                dve.wait_ge(wo_ps, s.n + 1)
                for t in range(TL):
                    v.bn_stats(st6[:, t, :], wbank[:, t * D:(t + 1) * D]).then_inc(lchain, 1)
                dve.wait_ge(lchain, s.n * 8 + TL)
                settle(dve)
                for t in range(TL):
                    v.bn_aggr(mv[:, t, :], st6[:, t, :]).then_inc(lchain, 1)

            def layer_shift(s, k):
                if has(k, 0, UNITS):
                    dve.wait_ge(lrs_sb, s.n + 1)
                    wait(dve, y_sb, s.n * TL)
                    v.scalar_tensor_tensor(out=lsh[:], in0=mv[:, :, 0], scalar=-1.0, in1=lrs[:],
                                           op0=ALU.mult, op1=ALU.mult).then_inc(lsh_sb, 1)

            def top_logits(s, k):
                if not has(k, 0, UNITS):
                    return
                dve.wait_ge(lg_ps, s.n + 1)
                settle(dve)
                for t in range(TL):
                    v.max(m8[:, t, :], lbank[:, t * E:(t + 1) * E]).then_inc(rchain, 1)

            def top_experts(s, k):
                if not has(k, 0, UNITS):
                    return
                dve.wait_ge(rchain, s.n * 9 + TL)
                wait(dve, ef_sb, s.n)
                settle(dve)
                for t in range(TL):
                    v.max_index(i8[:, t, :], m8[:, t, :], lbank[:, t * E:(t + 1) * E]).then_inc(rchain, 1)
                wait(dve, we_sb, s.n)
                v.tensor_tensor(wd[:], m8[:, :, 1], m8[:, :, 0], ALU.subtract).then_inc(wd_sb, 1)

            def one_hots(s, k):
                if not has(k, 0, UNITS):
                    return
                dve.wait_ge(rchain, s.n * 9 + 8)
                v.tensor_tensor(oneh[:], iota_e[:, 0:1, :].unsqueeze(1).to_broadcast([P, TL, 2, E]),
                                i8[:, :, 0:2].unsqueeze(3).to_broadcast([P, TL, 2, E]),
                                ALU.is_equal).then_inc(rchain, 1)

            def masks(s, k):
                if not has(k, 0, UNITS):
                    return
                dve.wait_ge(rchain, (s.n + 1) * 9)
                v.tensor_tensor(mask[:, s.par, 0:TL], oneh[:, :, 0, :], oneh[:, :, 1, :], ALU.add).then_inc(mask_sb, 1)

            def mask_sums(s, k):
                if not has(k, 0, UNITS):
                    return
                dve.wait_ge(mask_sb, s.n + 1)
                dve.wait_ge(carry_sb, s.n + 1)
                wait(dve, pos_ps, s.n)
                with nc.allow_low_precision(reason="counts up to TT are exact"):
                    v.tensor_reduce(mask[:, 1 - s.par, TL, :], mask[:, s.par].rearrange("p t e -> p e t"), AX.X,
                                    ALU.add).then_inc(carry_sb, 1)

            def weights_slots(s, k):
                if not has(k, 0, UNITS):
                    return
                dve.wait_ge(we_sb, s.n + 1)
                v.tensor_scalar(we1[:], we[:], 1.0, None, ALU.add).then_inc(wchain, 1)
                dve.wait_ge(pos_ps, s.n + 1)
                v.tensor_tensor(sbase[:], pbank.rearrange("p (t e) -> p t e", e=E),
                                iota_e[:, 1:2, :].to_broadcast([P, TL, E]), ALU.add).then_inc(schain, 1)
                dve.wait_ge(wchain, s.n * 2 + 1)
                v.reciprocal(w0[:], we1[:]).then_inc(wchain, 1)
                dve.wait_ge(schain, s.n * 2 + 1)
                v.tensor_tensor(sprod[:], oneh[:], sbase[:].unsqueeze(2).to_broadcast([P, TL, 2, E]), ALU.mult
                                ).then_inc(schain, 1)
                dve.wait_ge(wchain, s.n * 2 + 2)
                if k is None or k >= 2:
                    dve.wait_ge(scattered[s.par], s.half * (TL * 2 * 16))
                v.tensor_tensor(ys[:, s.par, :, F_W1], w0[:], we[:], ALU.mult).then_inc(field_sb, 1)
                dve.wait_ge(field_sb, s.n * 2 + 1)
                v.tensor_tensor(ys[:, s.par, :, F_DW], w0[:], ys[:, s.par, :, F_W1], ALU.subtract
                                ).then_inc(field_sb, 1)
                dve.wait_ge(schain, s.n * 2 + 2)
                with nc.allow_low_precision(reason="whole numbers"):
                    v.tensor_reduce(slot[:, s.par], sprod[:].rearrange("p t c e -> p (t c) e"), AX.X, ALU.add
                                    ).then_inc(slot_sb, 1)

            split_x(Step(0, 0), 0)
            v.tensor_tensor(wxp[:, 1, WV:], wx[:, WV:], wxp[:, 0, WV:].bitcast(F32), ALU.subtract
                            ).then_inc(setup_dve, 1)
            v.memset(mask[:, 0, TL, :], 0.0).then_inc(carry_sb, 1)
            v.tensor_copy(tri_b[:].rearrange("p a q -> p (a q)"), tri_f).then_inc(late_dve, 1)
            dve.wait_ge(setup_pool, 6)
            v.tensor_copy(iot[:], iot_i[:]).then_inc(late_dve, 1)
            v.tensor_copy(dest[:], dest_i[:]).then_inc(late_dve, 1)

            def body(s, k):
                k1, k2, kn = (None,) * 3 if k is None else (k - 1, k - 2, k + 1)
                log_sigmoid_d(s, k)
                layer_shift(s - 2, k2)
                keys_values(s, k, 0)
                log_sigmoid_z(s, k)
                scan(s, k, 0)
                keys_values(s, k, 1)
                head_sum(s - 1, k1)
                keys_values(s, k, 2)
                scan(s, k, 1)
                keys_values(s, k, 3)
                split_x(s + 1, kn)
                if k == UNITS + 1:
                    split_rest()
                top_logits(s - 2, k2)
                head_apply(s - 1, k1)
                top_experts(s - 2, k2)
                gates(s, k)
                scan(s, k, 2)
                one_hots(s - 2, k2)
                scan(s, k, 3)
                masks(s - 2, k2)
                apply_gate(s - 1, k1)
                mask_sums(s - 2, k2)
                weights_slots(s - 2, k2)
                layer_stats(s - 1, k1)
            steps(dve, *SA, body)

            n = [0]

            def link(ins):
                n[0] += 1
                ins.then_inc(tchain, 1)
                dve.wait_ge(tchain, n[0])

            def over_t(a):
                return a.unsqueeze(1).to_broadcast([P, TILES, E])

            def over_e(a):
                return a.unsqueeze(2).to_broadcast([P, TILES, E])

            dve.wait_ge(cnt_ps, 1)
            v.tensor_tensor(padi[:], obank[:, 0:E], iota_e[:, 1, :], ALU.add).then_inc(pad_sb, 1)
            link(v.tensor_scalar(cnti[:], obank[:, 0:E], float(TS - 1), None, ALU.add))
            link(v.tensor_scalar(cnts[:], cnti[:], TS.bit_length() - 1, None, ALU.arith_shift_right))
            link(v.tensor_copy(ntf[:], cnts[:]))
            link(v.tensor_tensor_scan(tend[:], iota_e[:, 2, :], ntf[:], 0.0, ALU.mult, ALU.add))
            link(v.scalar_tensor_tensor(out=tstep[:], in0=ntf[:], scalar=-float(TS), in1=iota_e[:, 3, :],
                                        op0=ALU.mult, op1=ALU.add))
            link(v.tensor_tensor(tge[:], over_e(iot[:]), over_t(tend[:]), ALU.is_ge))
            link(v.tensor_tensor(tgs[:], tge[:], over_t(tstep[:]), ALU.mult))
            v.tensor_reduce(texp[:], tge[:], AX.X, ALU.add).then_inc(tchain, 1)
            n[0] += 1
            link(v.tensor_reduce(trow[:], tgs[:], AX.X, ALU.add))
            link(v.scalar_tensor_tensor(out=trow[:], in0=iot[:], scalar=float(TS), in1=trow[:], op0=ALU.mult,
                                        op1=ALU.add))
            v.tensor_scalar(row_i[:], trow[:], float(DUMP), None, ALU.min).then_inc(table_sb, 1)
            v.tensor_scalar(exp_i[:], texp[:], float(E - 1), None, ALU.min).then_inc(table_sb, 1)
            dve.wait_ge(table_sb, 2)
            dve.wait_ge(w1lo_sb, E // 2)

            def copy_weights(s, k):
                if not has(k, 0, TILES):
                    return
                e = dve.value_load(exp_i[0:1, bass.ds(s.n, 1)], min_val=0, max_val=E - 1)
                wait(dve, h_ps, (s.n - 1) * 2)
                v.tensor_copy(wb1[:, s.par, 0, :], w1hi[:, bass.ds(e, 1), :].rearrange("p a f -> p (a f)"))
                v.tensor_copy(wb1[:, s.par, 1, :], w1lo[:, bass.ds(e, 1), :].rearrange("p a f -> p (a f)")
                              ).then_inc(bw_sb, 1)

            def split_rows(s, k):
                if not has(k, 0, TILES):
                    return
                bank = ps[:, 4 + 3 * s.par, 0:TS]
                dve.wait_ge(bx_ps, s.n + 1)
                wait(dve, h_ps, (s.n - 1) * 2)
                v.tensor_copy(xb[:, s.par, 0, :], bank).then_inc(bx_sb, 1)
                dve.wait_ge(bx_sb, s.n * 2 + 1)
                v.tensor_tensor(xb[:, s.par, 1, :], bank, xb[:, s.par, 0, :].bitcast(F32), ALU.subtract
                                ).then_inc(bx_sb, 1)

            def fields(s, k):
                if not has(k, 0, TILES):
                    return
                dve.wait_ge(rows_in[s.of(RB)], (s.turns(RB) + 1) * 16)
                wait(dve, field_read, s.n)
                v.tensor_scalar(fsel[:], xl[:, s.of(RB), :, F_EXPERT], texp[:, bass.ds(s.n, 1)], None, ALU.is_equal
                                ).then_inc(fchain, 1)
                dve.wait_ge(fchain, s.n * 3 + 1)
                v.tensor_tensor(fwd[:], fsel[:], xl[:, s.of(RB), :, F_DW], ALU.mult).then_inc(fchain, 1)
                dve.wait_ge(fchain, s.n * 3 + 2)
                wait(dve, yo_sb, (s.n - RB + 1) * ST)
                wait(dve, returned[s.of(RB)], s.turns(RB) * (ST * 16))
                v.tensor_tensor(fw[:, s.of(RB)], fwd[:], xl[:, s.of(RB), :, F_W1], ALU.add).then_inc(fchain, 1)
                v.scalar_tensor_tensor(out=fdst[:, s.of(RB)], in0=fsel[:], scalar=-float(TOKENS),
                                       in1=xl[:, s.of(RB), :, F_DEST], op0=ALU.mult, op1=ALU.add
                                       ).then_inc(field_read, 1)

            copy_weights(Step(0, 0, RB), 0)
            split_rows(Step(0, 0, RB), 0)

            def bodyb(s, k):
                kn = None if k is None else k + 1
                split_rows(s + 1, kn)
                copy_weights(s + 1, kn)
                fields(s, k)
            steps(dve, *SB, bodyb)

            def final_add(s, k):
                if has(k, 0, GROUPS):
                    dve.wait_ge(ya_sb, s.n + 1)
                    group = yres[:, bass.ds(s.n * CG, CG), :]
                    v.tensor_tensor(group, group, y0[:, s.of(RC)], ALU.add).then_inc(yr_sb, 1)

            def final_stats(s, k):
                if not has(k, 0, GROUPS):
                    return
                dve.wait_ge(yr_sb, s.n + 1)
                wait(dve, cchain, s.n * (2 * CG))
                settle(dve)
                for t in range(CG):
                    v.bn_stats(cs6[:, t, :], yres[:, bass.ds(s.n * CG + t, 1), :].rearrange("p a d -> p (a d)")
                               ).then_inc(cchain, 1)

            def final_aggr(s, k):
                if not has(k, 0, GROUPS):
                    return
                dve.wait_ge(cchain, s.n * (2 * CG) + CG)
                wait(dve, crs_sb, s.n - 1)
                wait(dve, csh_sb, s.n - 1)
                settle(dve)
                for t in range(CG):
                    v.bn_aggr(cmv[:, s.par, t, :], cs6[:, t, :]).then_inc(cchain, 1)

            def final_shift(s, k):
                if not has(k, 0, GROUPS):
                    return
                dve.wait_ge(crs_sb, s.n + 1)
                wait(dve, co_sb, (s.n - 1) * (CG - 1))
                v.scalar_tensor_tensor(out=csh[:, s.par], in0=cmv[:, s.par, :, 0], scalar=-1.0, in1=crs[:, s.par],
                                       op0=ALU.mult, op1=ALU.mult).then_inc(csh_sb, 1)
                last = yres[:, bass.ds(s.n * CG + CG - 1, 1), :].rearrange("p a d -> p (a d)")
                v.tensor_scalar(last, last, cmv[:, s.par, CG - 1, 0:1], crs[:, s.par, CG - 1:CG],
                                ALU.subtract, ALU.mult).then_inc(cl_sb, 1)

            def bodyc(s, k):
                k1, k2 = (None, None) if k is None else (k - 1, k - 2)
                final_add(s, k)
                final_stats(s - 1, k1)
                final_shift(s - 2, k2)
                final_aggr(s - 1, k1)
            steps(dve, 0, RC, GROUPS, GROUPS + 1, RC, bodyc)


_OUT = (P, TT, D)


def kernel(L0_attn_inputs, L0_attn_Wq, L0_attn_Wk, L0_attn_Wg1, L0_attn_Wg2, L0_attn_Wv, L0_attn_Wg, L0_attn_bg,
           L0_attn_Wo, L0_ffn_gate_w, L0_ffn_w1, L0_ffn_w2):
    import concourse.bacc as _bacc
    from concourse.bass_utils import run_bass_kernel_spmd as _run

    f32 = np.float32
    arrays = {
        "x": np.ascontiguousarray(np.asarray(L0_attn_inputs).reshape(UNITS, TL, P, D).transpose(0, 2, 1, 3)),
        "Wg2": np.ascontiguousarray(L0_attn_Wg2),
        "w1": np.ascontiguousarray(L0_ffn_w1),
        "w2": np.ascontiguousarray(L0_ffn_w2),
    }
    head_of_row = np.tile(np.repeat(np.arange(H), DK), 2)
    j_of_row = np.repeat(np.arange(2), HK)
    head_of_col, dv_of_col = np.repeat(np.arange(H), DV), np.tile(np.arange(DV), H)
    same_head = head_of_row[:, None, None] == head_of_col[None, None, :]
    same_dv = (2 * np.arange(G)[None, :, None] + j_of_row[:, None, None]) == dv_of_col[None, None, :]
    center = (same_head * (same_dv - 1.0 / DV)).astype(f32)
    triangle = np.stack([np.triu(np.ones((P, P), f32), 1), np.ones((P, P), f32)], 1)
    steps_ = np.where(np.arange(E) < E - 1, REGION, 2 * DUMP)
    numbers = np.broadcast_to(np.stack([np.arange(E), np.arange(E) * REGION, np.ones(E), steps_]).astype(f32),
                              (P, 4, E))

    def beside(widths, *parts):
        parts = [np.asarray(a).reshape(P, n) for a, n in zip(parts, widths.values(), strict=True)]
        return np.ascontiguousarray(np.concatenate(parts, 1))

    Wk, Wq = np.asarray(L0_attn_Wk), np.asarray(L0_attn_Wq)
    arrays["projections"] = np.ascontiguousarray(np.stack(
        [np.concatenate([Wk, Wk], 1), np.concatenate([Wq, Wq], 1), np.asarray(L0_attn_Wg)], 1))
    arrays["setup"] = beside(SETUP, np.eye(P, dtype=f32), L0_attn_Wg1,
                             np.asarray(L0_attn_Wv).reshape(D, H, G, 2).transpose(0, 2, 3, 1), L0_attn_bg)
    arrays["others"] = beside(OTHERS, center, triangle, numbers, L0_attn_Wo, np.asarray(L0_ffn_gate_w).T)
    nc = _bacc.Bacc("TRN2", target_bir_lowering=False, num_devices=1)
    aps = {n: nc.dram_tensor(n, a.shape, mybir.dt.from_np(a.dtype), kind="ExternalInput").ap()
           for n, a in arrays.items()}
    out = nc.dram_tensor("out", _OUT, F32, kind="ExternalOutput").ap()
    build(nc, out=out, **aps)
    r = _run(nc, [arrays], core_ids=[0])
    return r.results[0]["out"].transpose(1, 0, 2).reshape(np.asarray(L0_attn_inputs).shape)
```
